# Optimizing a Trainium2 kernel written in Bass

```python
import numpy as np
import jax
import jax.numpy as jnp

def _softmax(x, axis=-1):
    return jax.nn.softmax(x, axis=axis)

def _gelu(x):
    return jax.nn.gelu(x, approximate=True)

def _silu(x):
    return jax.nn.silu(x)

def _sigmoid(x):
    return jax.nn.sigmoid(x)

def _layernorm(x, axis=-1, eps=1e-05):
    m = jnp.mean(x, axis=axis, keepdims=True)
    v = jnp.var(x, axis=axis, keepdims=True)
    return (x - m) / jnp.sqrt(v + eps)

def _scatter_add(tgt, idx, src, axis=0):
    return tgt.at[idx].add(src)

def _segment_sum(src, seg, n):
    return jax.ops.segment_sum(src, seg, n)
kernel_name = 'mk_gnn_preln_d4_gnn_r8_8a4b7c'

def setup_inputs(seed: int=0):
    np.random.seed(seed)
    _w = jnp.asarray

    def _rec_inputs():
        import jax
        import jax.numpy as jnp
        _gk = jax.random.key(seed)
        x = -0.0007083 + 1.001 * jax.random.normal(jax.random.fold_in(_gk, 1), (6250, 48), jnp.float32)
        src = jax.random.randint(jax.random.fold_in(_gk, 2), (200000,), 0, 6250, jnp.int32)
        dst = jax.random.randint(jax.random.fold_in(_gk, 3), (200000,), 0, 6250, jnp.int32)
        _o = jnp.argsort(dst, stable=True)
        src = src[_o]
        dst = dst[_o]
        edge_attr_40 = jax.random.uniform(jax.random.fold_in(_gk, 12), (200000, 40), jnp.float32, 0.0, 1)
        edge_weight = jax.random.uniform(jax.random.fold_in(_gk, 14), (200000,), jnp.float32, 0.0, 7.99999)
        node_type_119 = jax.random.randint(jax.random.fold_in(_gk, 15), (6250,), 0, 119, jnp.int32)
        node_vec = jax.random.uniform(jax.random.fold_in(_gk, 16), (6250,), jnp.float32, 0.0, 3.99996)
        return (x, src, dst, edge_attr_40, edge_weight, node_type_119, node_vec)
    x, src, dst, edge_attr_40, edge_weight, node_type_119, node_vec = _rec_inputs()

    def _L0_gnn_setup():
        import jax, jax.numpy as jnp
        import numpy as np
        N = 6250
        E = 150000
        H = 48
        RBF = 40
        L = 4
        NELEM = 119
        G = 32
        CUT = 6.0

        def _ln(x, g, b):
            m = x.mean(-1, keepdims=True)
            v = ((x - m) ** 2).mean(-1, keepdims=True)
            return (x - m) * jax.lax.rsqrt(v + 1e-05) * g + b
        key = jax.random.key(seed)
        k = jax.random.split(key, 16)
        s = 0.1
        return {'h': jax.random.normal(k[0], (N, H), jnp.float32), 'edge_index': jax.random.randint(k[1], (2, E), 0, N), 'edge_attr': jax.random.uniform(k[2], (E, RBF), dtype=jnp.float32), 'distances': jax.random.uniform(k[3], (E,), dtype=jnp.float32) * 8.0, 'atom_z': jax.random.randint(k[4], (N,), 0, NELEM), 'node_mult': jax.random.uniform(k[5], (N,), dtype=jnp.float32) * 3.0 + 1.0, 'batch': jnp.sort(jax.random.randint(k[6], (N,), 0, 64)), 'Wq': jax.random.normal(k[7], (L, H, H), jnp.float32) * s, 'gq': jnp.ones((L, H), jnp.float32), 'bq': jnp.zeros((L, H), jnp.float32), 'Wk': jax.random.normal(k[8], (L, H, H), jnp.float32) * s, 'gk': jnp.ones((L, H), jnp.float32), 'bk': jnp.zeros((L, H), jnp.float32), 'Wm': jax.random.normal(k[9], (L, H, H), jnp.float32) * s, 'Wu': jax.random.normal(k[10], (L, 2 * H, H), jnp.float32) * s, 'go': jnp.ones((L, H), jnp.float32), 'bo': jnp.zeros((L, H), jnp.float32), 'F1W': jax.random.normal(k[11], (RBF, H), jnp.float32) * s, 'F1b': jnp.zeros((H,), jnp.float32), 'F2W': jax.random.normal(k[12], (H, H), jnp.float32) * s, 'F2b': jnp.zeros((H,), jnp.float32), 'gn': jnp.ones((H,), jnp.float32), 'bn': jnp.zeros((H,), jnp.float32), 'emb': jax.random.normal(k[13], (NELEM, G), jnp.float32) * 0.01, 'adapt': jax.random.normal(k[14], (G, G), jnp.float32) * 0.01}
    _L0_gnn_all = _L0_gnn_setup()
    _L0_gnn_in = {k: v for k, v in _L0_gnn_all.items() if k in ('Wq', 'gq', 'bq', 'Wk', 'gk', 'bk', 'Wm', 'Wu', 'go', 'bo', 'F1W', 'F1b', 'F2W', 'F2b', 'gn', 'bn', 'emb', 'adapt')}
    del _L0_gnn_all

    def _L1_gnn_setup():
        import jax, jax.numpy as jnp
        import numpy as np
        N_NODES = 12500
        N_EDGES = 200000
        D_IN = 48
        D_H = 48
        D_OUT = 48

        def _graph_conv(x, src, dst, w_rel, w_root, b, num_nodes):
            agg = jax.ops.segment_sum(x[src], dst, num_segments=num_nodes)
            return agg @ w_rel + x @ w_root + b
        key = jax.random.key(seed)
        ks = jax.random.split(key, 8)
        s = 0.05
        x = jax.random.normal(ks[0], (N_NODES, D_IN), dtype=jnp.float32)
        edge_index = jax.random.randint(ks[1], (2, N_EDGES), 0, N_NODES, dtype=jnp.int64)
        w_rel1 = jax.random.normal(ks[2], (D_IN, D_H), dtype=jnp.float32) * s
        w_root1 = jax.random.normal(ks[3], (D_IN, D_H), dtype=jnp.float32) * s
        b1 = jax.random.normal(ks[4], (D_H,), dtype=jnp.float32) * s
        w_rel2 = jax.random.normal(ks[5], (D_H, D_OUT), dtype=jnp.float32) * s
        w_root2 = jax.random.normal(ks[6], (D_H, D_OUT), dtype=jnp.float32) * s
        b2 = jax.random.normal(ks[7], (D_OUT,), dtype=jnp.float32) * s
        return {'x': x, 'edge_index': edge_index, 'w_rel1': w_rel1, 'w_root1': w_root1, 'b1': b1, 'w_rel2': w_rel2, 'w_root2': w_root2, 'b2': b2}
    _L1_gnn_all = _L1_gnn_setup()
    _L1_gnn_in = {k: v for k, v in _L1_gnn_all.items() if k in ('w_rel1', 'w_root1', 'b1', 'w_rel2', 'w_root2', 'b2')}
    del _L1_gnn_all

    def _L2_gnn_setup():
        import jax, jax.numpy as jnp
        import numpy as np
        CUTOFF = 6.0
        LN_EPS = 1e-05
        key = jax.random.key(seed)
        ks = jax.random.split(key, 16)
        N, E, H, R, NEL, G = (6250, 100000, 48, 40, 119, 32)
        inp = {'h': jax.random.normal(ks[0], (N, H), jnp.float32), 'edge_index': jax.random.randint(ks[1], (2, E), 0, N, jnp.int64), 'edge_attr': jax.random.uniform(ks[2], (E, R), jnp.float32), 'distances': jax.random.uniform(ks[3], (E,), jnp.float32) * 7.0, 'atom_z': jax.random.randint(ks[4], (N,), 0, NEL, jnp.int64), 'node_mult': jax.random.uniform(ks[5], (N,), jnp.float32) + 0.5, 'batch': jnp.zeros((N,), jnp.int64), 'W1': jax.random.normal(ks[6], (H, R), jnp.float32) / np.sqrt(R), 'b1': jax.random.normal(ks[7], (H,), jnp.float32) * 0.01, 'W2': jax.random.normal(ks[8], (H, H), jnp.float32) / np.sqrt(H), 'b2': jax.random.normal(ks[9], (H,), jnp.float32) * 0.01, 'emb': jax.random.normal(ks[10], (NEL, G), jnp.float32) * 0.01, 'adaptW': jax.random.normal(ks[11], (G, G), jnp.float32) * 0.01, 'gamma': jnp.ones((H,), jnp.float32), 'beta': jnp.zeros((H,), jnp.float32)}
        return inp
    _L2_gnn_all = _L2_gnn_setup()
    _L2_gnn_in = {k: v for k, v in _L2_gnn_all.items() if k in ('W1', 'b1', 'W2', 'b2', 'emb', 'adaptW', 'gamma', 'beta')}
    del _L2_gnn_all

    def _L3_gnn_setup():
        import jax, jax.numpy as jnp
        import numpy as np
        N_NODES = 12500
        N_EDGES = 200000
        C_IN = 48
        C_OUT = 48
        key = jax.random.key(seed)
        k_x, k_e, k_w = jax.random.split(key, 3)
        x = jax.random.normal(k_x, (N_NODES, C_IN), dtype=jnp.float32)
        edge_index = jax.random.randint(k_e, (2, N_EDGES), 0, N_NODES, dtype=jnp.int64)
        W = jax.random.normal(k_w, (C_IN, C_OUT), dtype=jnp.float32) * (1.0 / np.sqrt(C_IN))
        b = jnp.zeros((C_OUT,), dtype=jnp.float32)
        return {'x': x, 'edge_index': edge_index, 'W': W, 'b': b}
    _L3_gnn_all = _L3_gnn_setup()
    _L3_gnn_in = {k: v for k, v in _L3_gnn_all.items() if k in ('W', 'b')}
    del _L3_gnn_all
    return {'x': x, 'src': src, 'dst': dst, 'edge_attr_40': edge_attr_40, 'edge_weight': edge_weight, 'node_type_119': node_type_119, 'node_vec': node_vec, 'L0_gnn_Wq': _L0_gnn_in['Wq'], 'L0_gnn_gq': _L0_gnn_in['gq'], 'L0_gnn_bq': _L0_gnn_in['bq'], 'L0_gnn_Wk': _L0_gnn_in['Wk'], 'L0_gnn_gk': _L0_gnn_in['gk'], 'L0_gnn_bk': _L0_gnn_in['bk'], 'L0_gnn_Wm': _L0_gnn_in['Wm'], 'L0_gnn_Wu': _L0_gnn_in['Wu'], 'L0_gnn_go': _L0_gnn_in['go'], 'L0_gnn_bo': _L0_gnn_in['bo'], 'L0_gnn_F1W': _L0_gnn_in['F1W'], 'L0_gnn_F1b': _L0_gnn_in['F1b'], 'L0_gnn_F2W': _L0_gnn_in['F2W'], 'L0_gnn_F2b': _L0_gnn_in['F2b'], 'L0_gnn_gn': _L0_gnn_in['gn'], 'L0_gnn_bn': _L0_gnn_in['bn'], 'L0_gnn_emb': _L0_gnn_in['emb'], 'L0_gnn_adapt': _L0_gnn_in['adapt'], 'L1_gnn_w_rel1': _L1_gnn_in['w_rel1'], 'L1_gnn_w_root1': _L1_gnn_in['w_root1'], 'L1_gnn_b1': _L1_gnn_in['b1'], 'L1_gnn_w_rel2': _L1_gnn_in['w_rel2'], 'L1_gnn_w_root2': _L1_gnn_in['w_root2'], 'L1_gnn_b2': _L1_gnn_in['b2'], 'L2_gnn_W1': _L2_gnn_in['W1'], 'L2_gnn_b1': _L2_gnn_in['b1'], 'L2_gnn_W2': _L2_gnn_in['W2'], 'L2_gnn_b2': _L2_gnn_in['b2'], 'L2_gnn_emb': _L2_gnn_in['emb'], 'L2_gnn_adaptW': _L2_gnn_in['adaptW'], 'L2_gnn_gamma': _L2_gnn_in['gamma'], 'L2_gnn_beta': _L2_gnn_in['beta'], 'L3_gnn_W': _L3_gnn_in['W'], 'L3_gnn_b': _L3_gnn_in['b']}

def reference(x, src, dst, edge_attr_40, edge_weight, node_type_119, node_vec, L0_gnn_Wq, L0_gnn_gq, L0_gnn_bq, L0_gnn_Wk, L0_gnn_gk, L0_gnn_bk, L0_gnn_Wm, L0_gnn_Wu, L0_gnn_go, L0_gnn_bo, L0_gnn_F1W, L0_gnn_F1b, L0_gnn_F2W, L0_gnn_F2b, L0_gnn_gn, L0_gnn_bn, L0_gnn_emb, L0_gnn_adapt, L1_gnn_w_rel1, L1_gnn_w_root1, L1_gnn_b1, L1_gnn_w_rel2, L1_gnn_w_root2, L1_gnn_b2, L2_gnn_W1, L2_gnn_b1, L2_gnn_W2, L2_gnn_b2, L2_gnn_emb, L2_gnn_adaptW, L2_gnn_gamma, L2_gnn_beta, L3_gnn_W, L3_gnn_b):
    import jax
    import jax.numpy as jnp

    def _L0_gnn_ref(h, edge_index, edge_attr, distances, atom_z, node_mult, batch, Wq, gq, bq, Wk, gk, bk, Wm, Wu, go, bo, F1W, F1b, F2W, F2b, gn, bn, emb, adapt):
        import jax, jax.numpy as jnp
        import numpy as np
        N = 6250
        E = 150000
        H = 48
        RBF = 40
        L = 4
        NELEM = 119
        G = 32
        CUT = 6.0

        def _ln(x, g, b):
            m = x.mean(-1, keepdims=True)
            v = ((x - m) ** 2).mean(-1, keepdims=True)
            return (x - m) * jax.lax.rsqrt(v + 1e-05) * g + b
        src, dst = (edge_index[0], edge_index[1])
        gate = jax.nn.silu(edge_attr @ F1W + F1b) @ F2W + F2b
        ei = emb[atom_z[src]]
        ej = emb[atom_z[dst]]
        gate = gate + (ei * (ej @ adapt)).sum(-1, keepdims=True)
        cw = jnp.where(distances < CUT, 0.5 * (jnp.cos(jnp.pi * distances / CUT) + 1.0), 0.0)
        mj = node_mult[dst]
        msg = gate * h[dst] * (cw * mj)[:, None]
        agg = jax.ops.segment_sum(msg, src, num_segments=N)
        tot = jnp.clip(jax.ops.segment_sum(mj, src, num_segments=N), 1e-08, None)
        h = _ln(h + agg / tot[:, None], gn, bn)
        logm = jnp.log(jnp.clip(node_mult, 1.0, None))
        for i in range(L):
            Q = _ln(h @ Wq[i], gq[i], bq[i])
            K = _ln(h @ Wk[i], gk[i], bk[i])
            qi = Q[src]
            kj = K[dst]
            score = (qi * kj).sum(-1) + 0.1 * (edge_attr * qi[:, :RBF]).sum(-1) + logm[dst]
            smax = jax.ops.segment_max(score, src, num_segments=N)
            es = jnp.exp(jnp.minimum(score - smax[src], 20.0))
            denom = jax.ops.segment_sum(es, src, num_segments=N)
            alpha = es / (denom[src] + 1e-10)
            m = h[dst] @ Wm[i]
            aggi = jax.ops.segment_sum(alpha[:, None] * m, src, num_segments=N)
            z = jnp.concatenate([h, aggi], axis=-1) @ Wu[i]
            z = jnp.where(z > 0, z, 0.01 * z)
            h = _ln(h + z, go[i], bo[i])
        return h

    def _L1_gnn_ref(x, edge_index, w_rel1, w_root1, b1, w_rel2, w_root2, b2):
        import jax, jax.numpy as jnp
        import numpy as np
        N_NODES = 12500
        N_EDGES = 200000
        D_IN = 48
        D_H = 48
        D_OUT = 48

        def _graph_conv(x, src, dst, w_rel, w_root, b, num_nodes):
            agg = jax.ops.segment_sum(x[src], dst, num_segments=num_nodes)
            return agg @ w_rel + x @ w_root + b
        src, dst = (edge_index[0], edge_index[1])
        n = x.shape[0]
        h = jax.nn.relu(_graph_conv(x, src, dst, w_rel1, w_root1, b1, n))
        out = _graph_conv(h, src, dst, w_rel2, w_root2, b2, n)
        return out

    def _L2_gnn_ref(h, edge_index, edge_attr, distances, atom_z, node_mult, batch, W1, b1, W2, b2, emb, adaptW, gamma, beta):
        import jax, jax.numpy as jnp
        import numpy as np
        CUTOFF = 6.0
        LN_EPS = 1e-05
        src, dst = (edge_index[0], edge_index[1])
        N = h.shape[0]
        gate = jax.nn.silu(edge_attr @ W1.T + b1) @ W2.T + b2
        ei = emb[atom_z[src]]
        ej = emb[atom_z[dst]]
        adapt_logit = jnp.sum(ei * (ej @ adaptW.T), axis=-1, keepdims=True)
        gate = gate + adapt_logit
        cw = jnp.where(distances < CUTOFF, 0.5 * (jnp.cos(jnp.pi * distances / CUTOFF) + 1.0), 0.0)
        mj = node_mult[dst]
        msg = gate * h[dst] * (cw * mj)[:, None]
        agg = jax.ops.segment_sum(msg, src, num_segments=N)
        tot = jax.ops.segment_sum(mj, src, num_segments=N)
        agg = agg / jnp.clip(tot, 1e-08, None)[:, None]
        x = h + agg
        mu = jnp.mean(x, axis=-1, keepdims=True)
        var = jnp.mean(jnp.square(x - mu), axis=-1, keepdims=True)
        return (x - mu) / jnp.sqrt(var + LN_EPS) * gamma + beta

    def _L3_gnn_ref(x, edge_index, W, b):
        import jax, jax.numpy as jnp
        import numpy as np
        N_NODES = 12500
        N_EDGES = 200000
        C_IN = 48
        C_OUT = 48
        N = x.shape[0]
        loops = jnp.arange(N, dtype=edge_index.dtype)
        src = jnp.concatenate([edge_index[0], loops])
        dst = jnp.concatenate([edge_index[1], loops])
        deg = jax.ops.segment_sum(jnp.ones(src.shape, dtype=x.dtype), dst, num_segments=N)
        dinv = jnp.where(deg > 0, jax.lax.rsqrt(deg), 0.0)
        norm = dinv[src] * dinv[dst]
        h = x @ W
        msg = h[src] * norm[:, None]
        out = jax.ops.segment_sum(msg, dst, num_segments=N)
        return out + b
    edge_index = jnp.stack([src, dst])
    batch0 = jnp.zeros((6250,), jnp.int32)
    h = jnp.maximum(_layernorm(x, axis=-1), 0.0)
    x = x + _L0_gnn_ref(h, edge_index, edge_attr_40, edge_weight, node_type_119, node_vec, batch0, L0_gnn_Wq, L0_gnn_gq, L0_gnn_bq, L0_gnn_Wk, L0_gnn_gk, L0_gnn_bk, L0_gnn_Wm, L0_gnn_Wu, L0_gnn_go, L0_gnn_bo, L0_gnn_F1W, L0_gnn_F1b, L0_gnn_F2W, L0_gnn_F2b, L0_gnn_gn, L0_gnn_bn, L0_gnn_emb, L0_gnn_adapt)
    h = jnp.maximum(_layernorm(x, axis=-1), 0.0)
    x = x + _L1_gnn_ref(h, edge_index, L1_gnn_w_rel1, L1_gnn_w_root1, L1_gnn_b1, L1_gnn_w_rel2, L1_gnn_w_root2, L1_gnn_b2)
    h = jnp.maximum(_layernorm(x, axis=-1), 0.0)
    x = x + _L2_gnn_ref(h, edge_index, edge_attr_40, edge_weight, node_type_119, node_vec, batch0, L2_gnn_W1, L2_gnn_b1, L2_gnn_W2, L2_gnn_b2, L2_gnn_emb, L2_gnn_adaptW, L2_gnn_gamma, L2_gnn_beta)
    h = jnp.maximum(_layernorm(x, axis=-1), 0.0)
    x = x + _L3_gnn_ref(h, edge_index, L3_gnn_W, L3_gnn_b)
    return x

_drawn_inputs = setup_inputs


def setup_inputs(seed=0):
    import zlib

    import numpy as np

    out = dict(_drawn_inputs(seed))
    spreads = {'L0_gnn_gq': (1.0, 0.6),
     'L0_gnn_bq': (0.0, 0.8),
     'L0_gnn_gk': (1.0, 0.6),
     'L0_gnn_bk': (0.0, 2.0),
     'L0_gnn_go': (1.0, 0.2),
     'L0_gnn_bo': (0.0, 0.1),
     'L0_gnn_F1b': (0.0, 2.0),
     'L0_gnn_F2b': (0.0, 2.0),
     'L0_gnn_gn': (1.0, 0.2),
     'L0_gnn_bn': (0.0, 0.1),
     'L2_gnn_gamma': (1.0, 0.6),
     'L2_gnn_beta': (0.0, 2.0),
     'L3_gnn_b': (0.0, 2.0)}
    factors = {'edge_attr_40': 23.896,
     'edge_weight': 8.0,
     'node_vec': 81.755,
     'L0_gnn_F1W': 3.338,
     'L0_gnn_F2W': 3.386,
     'L0_gnn_emb': 200.0,
     'L0_gnn_adapt': 200.0,
     'L1_gnn_b1': 6.909,
     'L1_gnn_b2': 37.522,
     'L2_gnn_W1': 71.192,
     'L2_gnn_b1': 200.0,
     'L2_gnn_W2': 8.0,
     'L2_gnn_b2': 200.0,
     'L2_gnn_emb': 200.0,
     'L2_gnn_adaptW': 200.0,
     'L3_gnn_W': 2.76}
    for name, (base, spread) in spreads.items():
        noise = np.random.default_rng([zlib.crc32(name.encode()), seed]).standard_normal(out[name].shape)
        drawn = base * np.exp(spread * noise) if base else spread * noise
        out[name] = jnp.asarray(drawn.astype(out[name].dtype))
    for name, factor in factors.items():
        out[name] = (out[name] * factor).astype(out[name].dtype)
    return out
```

```python
from contextlib import ExitStack

import concourse.bass as bass
from concourse import mybir

F32 = mybir.dt.float32
BF16 = mybir.dt.bfloat16
I32 = mybir.dt.int32
ALU = mybir.AluOpType
ACT = mybir.ActivationFunctionType
AX = mybir.AxisListType

P = 128
N = 6250
E = 200000
H = 48
R = 40
G = 32
L = 4
CUT = 6.0
PI = 3.141592653589793

NB = -(-N // P)
LAST = N - (NB - 1) * P
GT = 2
GS = GT * P
RING = 8
NG = -(-((E + NB * (GS - 1)) // GS) // RING) * RING
NT = NG * GT
PAD = 255.0

EP, ET = 125, E // 125
SU = 8
SI = ET // (2 * SU)
RW = 44
C_W, C_KEY, C_IDX = R, R + 1, R + 2
XT = 104
TG, TA, TC = H + 1 + G, 2 * H + 2, H + 1
BIG = 1.0e30
NB7 = 7
W96 = 2 * H
PS_PAD = 64

LAYER_CHAIN = 32
PARAMS = 7 + 6 + 2 + 3 + 2 * 7 + 1
LAST_X = 2 + 3 * L + 1 + 1 + 2 + 1 + 1
LAYER_PROJ, LAYER_TURN, LAYER_LN, LAYER_X = 2, 1, 2, 3

assert NB == NB7 * NB7 and ET * EP == E and SI * 2 * SU == ET and NT % XT == 0 and NT % PS_PAD == 0


class Chain:

    def __init__(self, eng, sem):
        self.eng, self.sem, self.base, self.n = eng, sem, 0, 0

    def __call__(self, ins):
        self.n += 1
        ins.then_inc(self.sem, 1)
        self.eng.wait_ge(self.sem, self.base + self.n)


def again(eng, sem, base, g, ring):
    if isinstance(g, int) and g < ring:
        return
    eng.wait_ge(sem, base + g + 1 - ring)


def walk(eng, steps, depth):
    def turn(k, u):
        for lag, f in steps:
            if not isinstance(k, int) or 0 <= k - lag < NG:
                f(k - lag, (u - lag) % RING)

    for u in range(RING):
        turn(u, u)
    with eng.Fori(1, NG // RING) as i:
        for u in range(RING):
            turn(i * RING + u, u)
    for u in range(depth):
        turn(NG + u, u)


def build(nc, a, out):
    ctx = ExitStack()
    with ctx:
        def sb(name, shape, dt=F32):
            return ctx.enter_context(nc.sbuf_tensor(name, shape, dt))

        def sem(name):
            return ctx.enter_context(nc.semaphore(name))

        def dram(name, shape, dt=F32):
            return nc.dram_tensor(name, shape, dt, kind="Internal").ap()

        rec = dram("slot_records", [P, NT * RW])
        rec2 = dram("slot_pairs", [P, NT * 2])
        tab_g = dram("tab_gated", [NB * P, TG])
        tab_a = dram("tab_attention", [NB * P, TA])
        tab_c = dram("tab_conv", [NB * P, TC])
        rec_rows = rec.rearrange("p (t c) -> (p t) c", c=RW)
        rec2_rows = rec2.rearrange("p (t c) -> (p t) c", c=2)

        xs = sb("x_sum", [P, NB * H])
        z = sb("z", [P, NB * W96])
        yq = sb("yq", [P, NB * W96])
        tabs = sb("table_stage", [P, NB * TA])
        acc = sb("acc", [P, NB * TC])
        qt = sb("q_turned", [P, NB * P])
        emb = sb("emb_nodes", [P, NB * G])
        mult = sb("mult", [P, NB])
        logm = sb("log_mult", [P, NB])
        ztype = sb("node_type", [P, NB], I32)
        nmax = sb("neg_max", [P, NB])
        deg = sb("degree", [P, NB])
        ln_a, ln_b, ln_c, ln_d = (sb(f"ln_{c}", [P, 2 * NB]) for c in "abcd")
        idx_s = sb("idx_by_src", [P, NT + 2 * RING], I32)
        idx_d = sb("idx_by_dst", [P, NT + 2 * RING], I32)
        key_s = sb("key_by_src", [P, NT])
        cut_w = sb("cutoff", [P, NT])
        key_d = sb("key_by_dst", [P, NT])
        blk_s = sb("block_by_src", [1, NG], I32)
        blk_d = sb("block_by_dst", [1, NG], I32)
        rows = sb("gathered", [P, RING * GT * TA])
        ear = sb("edge_records", [P, RING * GT * RW])
        ids = sb("idx_stage", [P, RING * GT], I32)
        ring = sb("ring", [P, 8096])
        hot = ring[:, 0:RING * GS]
        nothot = ring[:, 0:4 * P].bitcast(BF16)
        prob = ring[:, 512:512 + 4 * GS]
        probt = ring[:, 1536:1536 + 4 * GS]
        kturn = ring[:, 2560:2560 + 4 * GS]
        qcur = ring[:, 3584:3584 + 4 * P]
        gmax = ring[:, 4096:4096 + RING]
        nmn = ring[:, 4104:4104 + RING]
        rdif = ring[:, 4112:4112 + RING]
        decay = ring[:, 4120:4120 + RING]
        hcut = ring[:, 2048:2048 + RING * GT * H]
        msg = ring[:, 2816:2816 + RING * GT * TC]
        eat = ring[:, 3600:3600 + 4 * GS]
        ebt = ring[:, 4624:4624 + 4 * GS]
        hid = ring[:, 5648:5648 + 4 * GS]
        logit = ring[:, 6672:6672 + RING * GT]
        junk = ring[:, 6688:6688 + 2 * GS].bitcast(BF16)
        xt_sb = ring[:, 7200:7200 + NB7 * P]
        pads = qt[:, ET:ET + 2 * NT]
        pair_l = tabs[:, 0:2 * NT].rearrange("p (t c) -> p t c", c=2)
        stage = ring[:, 3200:3200 + 2 * SU * RW].rearrange("p (u j c) -> p u j c", u=2, c=RW)
        stage_i = ring[:, 3904:3904 + 2 * SU].bitcast(I32).rearrange("p (u j) -> p u j", u=2)
        pair_e = ring[0:EP, 0:2 * ET].rearrange("p (t c) -> p t c", c=2)
        stage2 = ring[:, 3920:3920 + 4 * SU].rearrange("p (u j) -> p u j", u=2)
        stage2_i = ring[:, 3952:3952 + 2 * SU].bitcast(I32).rearrange("p (u j) -> p u j", u=2)
        w_e = qt[0:EP, 0:ET]
        krel_e = tabs[0:EP, 0:ET]
        oth_e = tabs[0:EP, ET:2 * ET]
        src_i = acc[0:EP, 0:ET].bitcast(I32)
        dst_i = tabs[0:EP, 2 * ET:3 * ET].bitcast(I32)
        row_s = xs[0:EP, 0:ET].bitcast(I32)
        row_d = idx_d[0:EP, 0:ET]
        bf, t1 = z[0:EP, 0:ET], z[0:EP, ET:2 * ET]
        t2, pos = yq[0:EP, 0:ET], yq[0:EP, ET:2 * ET]
        zero_e = cut_w[0:EP, 0:ET]
        cnt = sb("cnt", [P, NB])
        gf, incl, base = sb("gf", [P, NB]), sb("incl", [P, NB]), sb("base", [P, NB])
        gi = sb("gi", [P, NB], I32)
        iog, blf = z[0:1, 2 * ET:2 * ET + NG], yq[0:1, 2 * ET:2 * ET + NG]
        ioi = ring[:, 4000:4000 + NG].bitcast(I32)
        z1 = sb("zero_blocks", [P, NB])
        ident = sb("ident", [P, P])
        tri = sb("tri", [P, P])
        ones = sb("ones", [P, P])
        ioc = sb("iota_col", [P, P])
        neg_i = sb("neg_ident", [P, P], BF16)
        eps = sb("eps", [P, 1])
        half_pi = sb("half_pi", [P, 1])
        vec = {n: sb("v_" + n, [P, H]) for n in ("gn", "bn", "gamma", "beta", "b1", "b2", "b3")}
        lpar = sb("layer_vec", [P, L * 6 * H])
        lcur = sb("layer_cur", [P, 6 * H])
        wqk = sb("wqk", [H, L * W96])
        wqk_c = sb("wqk_c", [H, W96])
        ww = sb("ww", [W96, L * H])
        ww_c = sb("ww_c", [W96, H])
        wm_t = sb("wm_t", [H, L * H])
        wub = sb("wub", [H, L * H])
        wmu = sb("wmu", [H, L * H])
        f1 = [sb(f"f1_{k}", [R, H]) for k in range(2)]
        fb1 = [sb(f"fb1_{k}", [H, 1]) for k in range(2)]
        f2 = [sb(f"f2_{k}", [H + 1, H]) for k in range(2)]
        adp = [sb(f"adp_{k}", [G, G]) for k in range(2)]
        wc = [sb(f"wc_{k}", [W96, H]) for k in range(2)]
        w3 = sb("w3", [H, H])

        def blocks(t, w):
            return t[:, 0:NB * w].rearrange("p (b c) -> p b c", c=w)

        def ringv(t, n, w):
            return t.rearrange("p (s t c) -> p s t c", s=n, c=w)

        xs3, z3, yq3 = blocks(xs, H), blocks(z, W96), blocks(yq, W96)
        acc3, emb3 = blocks(acc, TC), blocks(emb, G)
        rows4 = ringv(rows[:, :], RING, TA)
        ear4 = ringv(ear[:, :], RING, RW)
        hot4, nothot4 = ringv(hot, RING, P), ringv(nothot, 4, P)
        hcut4, msg4 = ringv(hcut, RING, H), ringv(msg, RING, TC)

        ps = ctx.enter_context(nc.psum_tensor("ps", [P, 8 * 512], F32))
        psv = ps[:, :].rearrange("p (k n) -> p k n", n=512)
        ps_t, ps_s, ps_p, ps_a = (psv[:, 2 * k:2 * k + 2, :] for k in range(4))

        tick = {e: sem(f"tick_{e}") for e in ("pool", "act", "pe", "dve")}
        pads_ready, pads_stored, pairs_ready, pairs_stored = (sem(s) for s in (
            "pads_ready", "pads_stored", "pairs_ready", "pairs_stored"))
        ints_loaded, params_loaded, nodes_loaded, nodes_zeroed = (sem(s) for s in (
            "ints_loaded", "params_loaded", "nodes_loaded", "nodes_zeroed"))
        consts_ready, iota_ready, cols_ready = sem("consts_ready"), sem("iota_ready"), sem("cols_ready")
        counts_ready, sums_ready = sem("counts_ready"), sem("sums_ready")
        rows_placed, pairs_placed = sem("rows_placed"), sem("pairs_placed")
        rec_loaded = [sem(f"rec_loaded{u}") for u in range(2)]
        rec_staged = sem("rec_staged")
        scattered = [sem(f"scattered{u}") for u in range(2)]
        pair_staged = [sem(f"pair_staged{u}") for u in range(2)]
        pair_scattered = [sem(f"pair_scattered{u}") for u in range(2)]
        chunk_loaded = [sem(f"chunk_loaded{u}") for u in range(2)]
        chunk_used = sem("chunk_used")
        pairs_loaded = sem("pairs_loaded")
        emb_gathered = sem("emb_gathered")
        emb_used = sem("emb_used")
        wmu_made, wmu_copied, wmu_moved = sem("wmu_made"), sem("wmu_copied"), sem("wmu_moved")
        node_done = sem("node_done")
        ln_var, ln_std = sem("ln_var"), sem("ln_std")
        rec_parts, x_cleared, tabs_free = sem("rec_parts"), sem("x_cleared"), sem("tabs_free")
        angle_ready, cosine_done, degree_ready, degree_root = (sem(s) for s in (
            "angle_ready", "cosine_done", "degree_ready", "degree_root"))
        x_ready = sem("x_ready")
        proj_t, proj_evac, proj_mm, proj_out = (sem(s) for s in ("proj_t", "proj_evac", "proj_mm", "proj_out"))
        turn_t, turn_evac = sem("turn_t"), sem("turn_evac")
        table_ready, table_stored = sem("table_ready"), sem("table_stored")
        idx_staged = sem("idx_staged")
        gathered = [sem(f"gathered{s}") for s in range(RING)]
        ea_loaded = [sem(f"ea_loaded{s}") for s in range(RING)]
        conv = {n: sem("conv_" + n) for n in ("hot", "agg", "acc")}
        gate = {n: sem("gate_" + n) for n in (
            "hot", "hcut", "t", "evac", "evac_e", "mj", "hid", "bil", "act", "logit", "out", "msg", "agg", "acc")}
        att = {n: sem("att_" + n) for n in (
            "keys", "mask", "kt", "kt_evac", "q", "scores", "gmax", "nmn", "rdif", "saved",
            "decay", "probs", "pt", "pt_evac", "agg", "acc")}
        out_stored = sem("out_stored")

        def hold(eng, name, *waits):
            for s, v in waits:
                eng.wait_ge(s, v)
                eng.sem_inc(tick[name], 1)

        block = ctx.enter_context(nc.Block())

        @block.sync
        def _(sp):
            sp.dma_start(src_i, a["src"].rearrange("(p t) -> p t", p=EP)).then_inc(ints_loaded, 16)
            sp.dma_start(dst_i, a["dst"].rearrange("(p t) -> p t", p=EP)).then_inc(ints_loaded, 16)
            sp.dma_start(w_e, a["edge_weight"].rearrange("(p t) -> p t", p=EP)).then_inc(ints_loaded, 16)

            def par(dst, src):
                sp.dma_start(dst, src).then_inc(params_loaded, 16)

            for n, k in (("gn", "L0_gnn_gn"), ("bn", "L0_gnn_bn"), ("gamma", "L2_gnn_gamma"), ("beta", "L2_gnn_beta"),
                         ("b1", "L1_gnn_b1"), ("b2", "L1_gnn_b2"), ("b3", "L3_gnn_b")):
                par(vec[n][:, :], a[k].partition_broadcast(P))
            lp = lpar[:, :].rearrange("p (l k c) -> p l k c", l=L, c=H)
            for j, k in enumerate(("gq", "gk", "bq", "bk", "go", "bo")):
                par(lp[:, :, j, :], a["L0_gnn_" + k].partition_broadcast(P))
            wq3 = wqk[:, :].rearrange("p (l c) -> p l c", l=L)
            par(wq3[:, :, 0:H], a["L0_gnn_Wq"].rearrange("l k c -> k l c"))
            par(wq3[:, :, H:W96], a["L0_gnn_Wk"].rearrange("l k c -> k l c"))
            par(ww[0:H, :].rearrange("p (l c) -> p l c", l=L), a["L0_gnn_Wu"][:, 0:H, :].rearrange("l k c -> k l c"))
            par(wub[:, :].rearrange("p (l c) -> p l c", l=L), a["L0_gnn_Wu"][:, H:W96, :].rearrange("l k c -> k l c"))
            par(wm_t[:, :].rearrange("p (l c) -> p l c", l=L), a["Wm_t"].rearrange("l k c -> k l c"))
            for k, (w1, b1, w2, b2, ad) in enumerate((
                    ("L0_gnn_F1W", "L0_gnn_F1b", "L0_gnn_F2W", "L0_gnn_F2b", "adapt_t"),
                    ("W1_t", "L2_gnn_b1", "W2_t", "L2_gnn_b2", "L2_gnn_adaptW"))):
                par(f1[k][:, :], a[w1])
                par(fb1[k][:, :], a[b1].rearrange("(c k) -> c k", k=1))
                par(f2[k][0:H, :], a[w2])
                par(f2[k][H:H + 1, :], a[b2].rearrange("(k c) -> k c", k=1))
                par(adp[k][:, :], a[ad])
                par(wc[k][0:H, :], a[f"L1_gnn_w_root{k + 1}"])
                par(wc[k][H:W96, :], a[f"L1_gnn_w_rel{k + 1}"])
            par(w3[:, :], a["L3_gnn_W"])
            sp.wait_ge(nodes_zeroed, 2)
            for dst, src in ((mult, a["node_vec"]), (ztype, a["node_type_119"])):
                sp.dma_start(dst[:, 0:NB - 1], src[0:(NB - 1) * P].rearrange("(b p) -> p b", p=P), allow_slow_non_contiguous=True).then_inc(nodes_loaded, 16)
                sp.dma_start(dst[0:LAST, NB - 1:NB], src[(NB - 1) * P:N].rearrange("(p k) -> p k", k=1)).then_inc(nodes_loaded, 16)
            sp.wait_ge(pads_ready, 1)
            for c in range(NT // PS_PAD):
                sp.dma_start(rec[:, c * PS_PAD * RW:(c + 1) * PS_PAD * RW], pads[:, 0:PS_PAD * RW]).then_inc(pads_stored, 16)
            sp.wait_ge(pairs_ready, 1)
            sp.dma_start(rec2, pads).then_inc(pairs_stored, 16)
            sp.wait_ge(wmu_copied, 1)
            sp.dma_start(ww[H:W96, :], wmu[:, :]).then_inc(wmu_moved, 16)

            ea = a["edge_attr_40"].rearrange("(p t) c -> p t c", p=EP)

            def load_ea(i, u):
                if not (isinstance(i, int) and i == 0):
                    sp.wait_ge(scattered[u], i * (16 * SU))
                sp.dma_start(stage[0:EP, u, :, 0:R], ea[:, bass.ds(i * (2 * SU) + u * SU, SU), :]).then_inc(rec_loaded[u], 16)

            sp.wait_ge(node_done, 1)
            for u in range(2):
                load_ea(0, u)
            with sp.Fori(1, SI) as i:
                for u in range(2):
                    load_ea(i, u)
            pair_cols = ring[0:EP, 0:2 * ET]

            def load_pairs(i, u):
                if not (isinstance(i, int) and i == 0):
                    sp.wait_ge(pair_scattered[u], i * (16 * SU))
                sp.dma_start(stage2_i[0:EP, u, :], row_d[:, bass.ds(i * (2 * SU) + u * SU, SU)]).then_inc(pair_staged[u], 16)
                sp.dma_start(stage2[0:EP, u, :], pair_cols[:, bass.ds((i * (2 * SU) + u * SU) * 2, 2 * SU)]).then_inc(pair_staged[u], 16)

            sp.wait_ge(pairs_placed, 1)
            for u in range(2):
                load_pairs(0, u)
            for u in range(2):
                sp.wait_ge(scattered[u], SI * SU * 16)
            for c in range(NT // XT):
                if c >= 2:
                    sp.wait_ge(chunk_used, c - 1)
                sp.dma_start((z, yq)[c % 2][:, 0:XT * RW], rec[:, c * XT * RW:(c + 1) * XT * RW]).then_inc(chunk_loaded[c % 2], 16)
            with sp.Fori(1, SI) as i:
                for u in range(2):
                    load_pairs(i, u)
            for u in range(2):
                sp.wait_ge(pair_scattered[u], SI * SU * 16)
            sp.wait_ge(x_cleared, 1)
            sp.dma_start(xs3[:, 0:NB - 1, :], a["x"][0:(NB - 1) * P, :].rearrange("(b p) c -> p b c", p=P)).then_inc(nodes_loaded, 16)
            sp.dma_start(xs3[0:LAST, NB - 1, :], a["x"][(NB - 1) * P:N, :]).then_inc(nodes_loaded, 16)

            def store_table(tab, w, n):
                sp.wait_ge(table_ready, n)
                sp.dma_start(tab.rearrange("(b p) c -> p b c", p=P), blocks(tabs, w)).then_inc(table_stored, 16)

            def load_edges(base, pass_no, used):
                def step(g, s):
                    again(sp, used, base, g, RING)
                    sp.dma_start(ear[:, s * GT * RW:(s + 1) * GT * RW],
                                 rec[:, bass.ds(g * (GT * RW), GT * RW)]).then_inc(ea_loaded[s], 16)
                walk(sp, [(0, step)], 0)

            store_table(tab_g, TG, 1)
            load_edges(0, 0, gate["t"])
            with sp.Fori(0, L) as l:
                store_table(tab_a, TA, l + 2)
                load_edges(l * NG, l + 1, att["keys"])
            sp.wait_ge(tabs_free, 1)
            sp.dma_start(tabs[:, 0:2 * NT], rec2).then_inc(pairs_loaded, 16)
            store_table(tab_c, TC, L + 2)
            store_table(tab_c, TC, L + 3)
            store_table(tab_g, TG, L + 4)
            load_edges(NG, L + 1, gate["t"])
            store_table(tab_c, TC, L + 5)
            sp.wait_ge(x_ready, LAST_X)
            sp.dma_start(out[0:(NB - 1) * P, :].rearrange("(b p) c -> p b c", p=P), xs3[:, 0:NB - 1, :]).then_inc(out_stored, 16)
            sp.dma_start(out[(NB - 1) * P:N, :], xs3[0:LAST, NB - 1, :]).then_inc(out_stored, 16)
            sp.wait_ge(out_stored, 32)

        @block.gpsimd
        def _(pool):
            pool.iota(ioi, pattern=[[1, NG]], base=0, channel_multiplier=0).then_inc(iota_ready, 1)
            pool.memset(ones[:, :], 1.0).then_inc(consts_ready, 1)
            pool.memset(ident[:, :], 0.0).then_inc(consts_ready, 1)
            pool.memset(neg_i[:, :], 0.0).then_inc(consts_ready, 1)
            pool.memset(tri[:, :], 1.0).then_inc(consts_ready, 1)
            pool.memset(mult[:, :], 1.0).then_inc(nodes_zeroed, 1)
            pool.memset(ztype[:, :], 0).then_inc(nodes_zeroed, 1)
            pool.wait_ge(consts_ready, 4)
            pool.affine_select(out=ident[:, :], in_=ident[:, :], compare_op=ALU.not_equal, fill=1.0, base=0,
                               pattern=[[-1, P]], channel_multiplier=1).then_inc(consts_ready, 1)
            pool.affine_select(out=neg_i[:, :], in_=neg_i[:, :], compare_op=ALU.not_equal, fill=-BIG, base=0,
                               pattern=[[-1, P]], channel_multiplier=1).then_inc(consts_ready, 1)
            pool.affine_select(out=tri[:, :], in_=tri[:, :], compare_op=ALU.is_gt, fill=0.0, base=0,
                               pattern=[[1, P]], channel_multiplier=-1).then_inc(consts_ready, 1)

            def gather_emb(table):
                for b in range(NB):
                    pool.indirect_dma_start(out=emb3[:, b, :], out_offset=None, in_=table,
                                            in_offset=bass.IndirectOffsetOnAxis(ap=ztype[:, b:b + 1], axis=0)).then_inc(emb_gathered, 16)

            pool.wait_ge(nodes_loaded, 64)
            gather_emb(a["L0_gnn_emb"])

            def scatter(i, u):
                hold(pool, "pool", (rec_loaded[u], (i + 1) * 16), (rec_staged, i * 2 + u + 1))
                for j in range(SU):
                    pool.indirect_dma_start(out=rec_rows, out_offset=bass.IndirectOffsetOnAxis(ap=stage_i[0:EP, u, j:j + 1], axis=0),
                                            in_=stage[0:EP, u, j, :], in_offset=None).then_inc(scattered[u], 16)

            pool.wait_ge(pads_stored, 16 * (NT // PS_PAD))
            for u in range(2):
                scatter(0, u)
            with pool.Fori(1, SI) as i:
                for u in range(2):
                    scatter(i, u)

            def scatter2(i, u):
                hold(pool, "pool", (pair_staged[u], (i + 1) * 32))
                for j in range(SU):
                    pool.indirect_dma_start(out=rec2_rows, out_offset=bass.IndirectOffsetOnAxis(ap=stage2_i[0:EP, u, j:j + 1], axis=0),
                                            in_=stage2[0:EP, u, 2 * j:2 * j + 2], in_offset=None).then_inc(pair_scattered[u], 16)

            pool.wait_ge(pairs_stored, 16)
            for u in range(2):
                scatter2(0, u)
            with pool.Fori(1, SI) as i:
                for u in range(2):
                    scatter2(i, u)

            def gather(tab, w, pass_no):
                hold(pool, "pool", (table_stored, (pass_no + 1) * 16))
                base = pass_no * (NG + 1)

                def step(g, s):
                    n = base + 1 if isinstance(g, int) and g < RING else base + g - RING + 2
                    hold(pool, "pool", (idx_staged, n))
                    for t in range(GT):
                        pool.indirect_dma_start(out=rows4[:, s, t, 0:w], out_offset=None, in_=tab,
                                                in_offset=bass.IndirectOffsetOnAxis(ap=ids[:, s * GT + t:s * GT + t + 1], axis=0)).then_inc(gathered[s], 16)
                walk(pool, [(0, step)], 0)

            gather(tab_g, TG, 0)
            with pool.Fori(0, L) as l:
                gather(tab_a, TA, l + 1)
            pool.wait_ge(emb_used, 1)
            gather_emb(a["L2_gnn_emb"])
            gather(tab_c, TC, L + 1)
            gather(tab_c, TC, L + 2)
            gather(tab_g, TG, L + 3)
            gather(tab_c, TC, L + 4)

        def got(pass_no, g, s):
            return (pass_no * (NG // RING) + 1) * (16 * GT) + ((g - s) * (16 * GT // RING) if not isinstance(g, int) else (g - s) // RING * (16 * GT))

        def got_ea(pass_no, g, s):
            return (pass_no * (NG // RING) + 1) * 16 + ((g - s) * (16 // RING) if not isinstance(g, int) else (g - s) // RING * 16)

        @block.scalar
        def _(act):
            def put(i, u):
                if not (isinstance(i, int) and i == 0):
                    hold(act, "act", (scattered[u], i * (16 * SU)))
                cols = bass.ds(i * (2 * SU) + u * SU, SU)
                act.activation(stage_i[0:EP, u, :], row_s[:, cols], ACT.Copy).then_inc(rec_parts, 1)
                act.activation(stage[0:EP, u, :, C_W], w_e[:, cols], ACT.Copy).then_inc(rec_parts, 1)
                act.activation(stage[0:EP, u, :, C_KEY], krel_e[:, cols], ACT.Copy).then_inc(rec_parts, 1)
                act.activation(stage[0:EP, u, :, C_IDX], oth_e[:, cols], ACT.Copy).then_inc(rec_parts, 1)
                act.wait_ge(rec_parts, i * 8 + 4 * u + 4)
                act.sem_inc(rec_staged, 1)

            act.wait_ge(params_loaded, PARAMS * 16)
            act.wait_ge(cols_ready, 2)
            act.wait_ge(wmu_made, 1)
            act.activation(wmu[:, :], ps_s[0:H, 0, 0:L * H], ACT.Copy).then_inc(wmu_copied, 1)
            act.wait_ge(rows_placed, 1)
            for u in range(2):
                put(0, u)
            with act.Fori(1, SI) as i:
                for u in range(2):
                    put(i, u)

            class At:
                ln = proj = turn = 0

            def std(n):
                act.wait_ge(ln_var, At.ln + 1)
                act.activation(ln_c[:, 0:n], ln_b[:, 0:n], ACT.Sqrt, bias=eps[:, 0:1], scale=1.0 / H).then_inc(ln_std, 1)
                At.ln = At.ln + 1

            def project(k):
                b0 = At.proj * NB7
                with act.Fori(0, NB7) as j:
                    act.wait_ge(proj_t, b0 + j + 1)
                    act.activation(xt_sb[0:k, :], ps[0:k, 0:NB7 * P], ACT.Copy).then_inc(proj_evac, 1)
                At.proj = At.proj + 1

            def turned(k):
                b0 = At.turn * NB7
                with act.Fori(0, NB7) as j:
                    hold(act, "act", (turn_t, b0 + j + 1))
                    act.activation(qt[0:k, bass.ds(j * (NB7 * P), NB7 * P)], ps[0:k, 0:NB7 * P], ACT.Copy).then_inc(turn_evac, 1)
                hold(act, "act", (turn_evac, b0 + NB7))
                At.turn = At.turn + 1

            act.wait_ge(angle_ready, 1)
            act.activation(cut_w[:, :], cut_w[:, :], ACT.Sin, bias=half_pi[:, 0:1], scale=-PI / CUT).then_inc(cosine_done, 1)
            act.activation(logm[:, :], logm[:, :], ACT.Ln).then_inc(cosine_done, 1)

            def gated(c):
                base = c * NG

                def evac(g, s):
                    r, par = s % 4, s % 2
                    act.wait_ge(gate["t"], base + g + 1)
                    act.activation(eat[0:R, r * GS:(r + 1) * GS], ps_t[0:R, par, 0:GS], ACT.Copy).then_inc(gate["evac"], 1)
                    act.activation(ebt[0:G, r * GS:(r + 1) * GS], ps_t[0:G, par, GS:2 * GS], ACT.Copy).then_inc(gate["evac_e"], 1)
                    again(act, gate["agg"], base, g, RING)
                    act.activation(msg4[:, s, :, H], rows4[:, s, :, H], ACT.Copy).then_inc(gate["mj"], 1)

                def silu(g, s):
                    r, par = s % 4, s % 2
                    act.wait_ge(gate["hid"], base + g + 1)
                    again(act, gate["out"], base, g, 4)
                    act.activation(hid[0:H, r * GS:(r + 1) * GS], ps_s[0:H, par, 0:GS], ACT.Silu,
                                   bias=fb1[c][:, 0:1]).then_inc(gate["act"], 1)

                walk(act, [(0, evac), (2, silu)], 2)

            def attention(base):
                def evac(g, s):
                    r, par = s % 4, s % 2
                    b = act.value_load(blk_s[0:1, bass.ds(g, 1)], min_val=0, max_val=NB - 1)
                    act.activation(qcur[0:H + 1, r * P:(r + 1) * P], qt[0:H + 1, bass.ds(b * P, P)], ACT.Copy).then_inc(att["q"], 1)
                    act.wait_ge(att["kt"], base + g + 1)
                    act.activation(kturn[0:H + 1, r * GS:(r + 1) * GS], ps_t[0:H + 1, par, 0:GS], ACT.Copy).then_inc(att["kt_evac"], 1)

                def exps(g, s):
                    r, par = s % 4, s % 2
                    act.wait_ge(att["rdif"], base + g + 1)
                    act.activation(decay[:, s:s + 1], rdif[:, s:s + 1], ACT.Exp).then_inc(att["decay"], 1)
                    act.activation(prob[:, r * GS:(r + 1) * GS], ps_s[:, par, 0:GS], ACT.Exp,
                                   bias=nmn[:, s:s + 1]).then_inc(att["probs"], 1)

                def back(g, s):
                    r, par = s % 4, s % 2
                    act.wait_ge(att["pt"], base + g + 1)
                    again(act, att["agg"], base, g, 4)
                    act.activation(probt[:, r * GS:(r + 1) * GS], ps_p[:, par, 0:GS], ACT.Copy).then_inc(att["pt_evac"], 1)

                walk(act, [(0, evac), (2, exps), (3, back)], 3)

            project(G)
            turned(G)
            std(NB)
            gated(0)
            std(NB)
            p0, t0, n0 = At.proj, At.turn, At.ln
            with act.Fori(0, L) as l:
                At.proj, At.turn, At.ln = l * LAYER_PROJ + p0, l * LAYER_TURN + t0, l * LAYER_LN + n0
                project(H)
                std(2 * NB)
                turned(H)
                attention(l * NG)
                project(W96)
                std(NB)
            At.proj, At.turn, At.ln = L * LAYER_PROJ + p0, L * LAYER_TURN + t0, L * LAYER_LN + n0
            std(NB)
            project(W96)
            project(W96)
            project(G)
            turned(G)
            std(NB)
            gated(1)
            std(NB)
            std(NB)
            act.wait_ge(degree_ready, 1)
            act.activation(deg[:, :], deg[:, :], ACT.Sqrt).then_inc(degree_root, 1)
            project(H)

        @block.tensor
        def _(pe):
            pe.wait_ge(consts_ready, 7)
            pe.wait_ge(params_loaded, PARAMS * 16)
            for l in range(L):
                last = pe.matmul(ps_s[0:H, 0, l * H:(l + 1) * H], wm_t[:, l * H:(l + 1) * H], wub[:, l * H:(l + 1) * H],
                                 start=True, stop=True)
            last.then_inc(wmu_made, 1)
            for n in range(2):
                pe.wait_ge(counts_ready, n + 1)
                pe.matmul(ps_p[:, 0, 0:NB], ones[0:EP, :], cnt[0:EP, :], start=True, stop=True)
                pe.matmul(ps_p[0:EP, 1, 0:NB], tri[0:EP, 0:EP], cnt[0:EP, :], start=True, stop=True).then_inc(sums_ready, 1)

            class At:
                x = proj = turn = 0

            def turn_blocks(src, j):
                for i in range(NB7):
                    last = pe.transpose(ps[0:W96, i * P:(i + 1) * P], src[:, (j * NB7 + i) * W96:(j * NB7 + i + 1) * W96], ident[:, :])
                return last

            def project(src, k, w, n):
                hold(pe, "pe", (x_ready, At.x + 1))
                b0 = At.proj * NB7
                for j in range(NB7):
                    turn_blocks(src, j).then_inc(proj_t, 1)
                    pe.wait_ge(proj_evac, b0 + j + 1)
                    for i in range(NB7):
                        last = pe.matmul(ps[:, 4 * 512 + i * P:4 * 512 + i * P + n], xt_sb[0:k, i * P:(i + 1) * P], w,
                                         start=True, stop=True)
                    last.then_inc(proj_mm, 1)
                    hold(pe, "pe", (proj_out, b0 + j + 1))
                At.proj, At.x = At.proj + 1, At.x + 1

            def turned(src):
                hold(pe, "pe", (x_ready, At.x + 1))
                b0 = At.turn * NB7
                for j in range(NB7):
                    turn_blocks(src, j).then_inc(turn_t, 1)
                    hold(pe, "pe", (turn_evac, b0 + j + 1))
                At.turn, At.x = At.turn + 1, At.x + 1

            def gated(c, pass_no):
                base = c * NG

                def turn(g, s):
                    par = s % 2
                    pe.wait_ge(gathered[s], got(pass_no, g, s))
                    pe.wait_ge(ea_loaded[s], got_ea((0, L + 1)[c], g, s))
                    again(pe, gate["evac_e"], base, g, 2)
                    pe.sem_inc(tick["pe"], 1)
                    for t in range(GT):
                        pe.transpose(ps_t[0:R, par, t * P:(t + 1) * P], ear4[:, s, t, 0:R], ident[:, :])
                    for t in range(GT):
                        last = pe.transpose(ps_t[0:G, par, GS + t * P:GS + (t + 1) * P], rows4[:, s, t, H + 1:TG], ident[:, :])
                    last.then_inc(gate["t"], 1)

                def first(g, s):
                    r, par = s % 4, s % 2
                    b = pe.value_load(blk_s[0:1, bass.ds(g, 1)], min_val=0, max_val=NB - 1)
                    pe.wait_ge(gate["evac"], base + g + 1)
                    again(pe, gate["act"], base, g, 2)
                    pe.sem_inc(tick["pe"], 1)
                    pe.matmul(ps_s[0:H, par, 0:GS], f1[c][:, :], eat[0:R, r * GS:(r + 1) * GS],
                              start=True, stop=True).then_inc(gate["hid"], 1)
                    hold(pe, "pe", (gate["evac_e"], base + g + 1))
                    if not (isinstance(g, int) and g < 2):
                        hold(pe, "pe", (gate["logit"], base + g - 1))
                    for t in range(GT):
                        last = pe.matmul(ps_p[:, par, t * P:(t + 1) * P], ebt[0:G, r * GS + t * P:r * GS + (t + 1) * P],
                                         qt[0:G, bass.ds(b * P, P)], start=True, stop=True)
                    last.then_inc(gate["bil"], 1)

                def second(g, s):
                    r, par = s % 4, s % 2
                    pe.wait_ge(gate["act"], base + g + 1)
                    again(pe, gate["msg"], base, g, 2)
                    for t in range(GT):
                        last = pe.matmul(ps_a[:, par, P + t * H:P + (t + 1) * H], hid[0:H + 1, r * GS + t * P:r * GS + (t + 1) * P],
                                         f2[c][:, :], start=True, stop=True)
                    last.then_inc(gate["out"], 1)

                def total(g, s):
                    par = s % 2
                    pe.wait_ge(gate["msg"], base + g + 1)
                    pe.wait_ge(gate["mj"], base + g + 1)
                    again(pe, gate["acc"], base, g, 2)
                    for t in range(GT):
                        last = pe.matmul(ps_a[:, par, 0:TC], hot4[:, s, t, :], msg4[:, s, t, :], start=t == 0, stop=t == GT - 1)
                    last.then_inc(gate["agg"], 1)

                walk(pe, [(5, total), (3, second), (0, turn), (1, first)], 5)

            def attention(base, pass_no):
                def turn(g, s):
                    par = s % 2
                    pe.wait_ge(att["keys"], base + g + 1)
                    again(pe, att["kt_evac"], base, g, 2)
                    pe.sem_inc(tick["pe"], 1)
                    for t in range(GT):
                        last = pe.transpose(ps_t[0:H + 1, par, t * P:(t + 1) * P], rows4[:, s, t, 0:H + 1], ident[:, :])
                    last.then_inc(att["kt"], 1)

                def scores(g, s):
                    r, par = s % 4, s % 2
                    pe.wait_ge(att["q"], base + g + 1)
                    pe.wait_ge(att["kt_evac"], base + g + 1)
                    pe.wait_ge(att["mask"], base + g + 1)
                    again(pe, att["probs"], base, g, 2)
                    for t in range(GT):
                        pe.matmul(ps_s[:, par, t * P:(t + 1) * P], qcur[0:H + 1, r * P:(r + 1) * P],
                                  kturn[0:H + 1, r * GS + t * P:r * GS + (t + 1) * P], start=True, stop=False)
                        last = pe.matmul(ps_s[:, par, t * P:(t + 1) * P], nothot4[:, r, t, :], neg_i[:, :],
                                         start=False, stop=True)
                    last.then_inc(att["scores"], 1)

                def back(g, s):
                    r, par = s % 4, s % 2
                    pe.wait_ge(att["probs"], base + g + 1)
                    again(pe, att["pt_evac"], base, g, 2)
                    for t in range(GT):
                        last = pe.transpose(ps_p[:, par, t * P:(t + 1) * P], prob[:, r * GS + t * P:r * GS + (t + 1) * P], ident[:, :])
                    last.then_inc(att["pt"], 1)

                def total(g, s):
                    r, par = s % 4, s % 2
                    pe.wait_ge(att["pt_evac"], base + g + 1)
                    again(pe, att["acc"], base, g, 2)
                    for t in range(GT):
                        last = pe.matmul(ps_a[:, par, 0:TC], probt[:, r * GS + t * P:r * GS + (t + 1) * P],
                                         rows4[:, s, t, H + 1:TA], start=t == 0, stop=t == GT - 1)
                    last.then_inc(att["agg"], 1)

                walk(pe, [(3, back), (0, turn), (1, scores), (4, total)], 4)

            def summed(c, pass_no):
                base = c * NG

                def total(g, s):
                    par = s % 2
                    pe.wait_ge(gathered[s], got(pass_no, g, s))
                    pe.wait_ge(conv["hot"], base + g + 1)
                    again(pe, conv["acc"], base, g, 2)
                    for t in range(GT):
                        last = pe.matmul(ps_a[:, par, 0:TC], hot4[:, s, t, :], rows4[:, s, t, 0:TC], start=t == 0, stop=t == GT - 1)
                    last.then_inc(conv["agg"], 1)

                walk(pe, [(1, total)], 1)

            project(z, G, adp[0][:, :], G)
            turned(yq)
            gated(0, 0)
            p0, t0, x0 = At.proj, At.turn, At.x
            with pe.Fori(0, L) as l:
                At.proj, At.turn, At.x = l * LAYER_PROJ + p0, l * LAYER_TURN + t0, l * LAYER_X + x0
                project(z, H, wqk_c[:, :], W96)
                turned(yq)
                attention(l * NG, l + 1)
                project(z, W96, ww_c[:, :], H)
            At.proj, At.turn, At.x = L * LAYER_PROJ + p0, L * LAYER_TURN + t0, L * LAYER_X + x0
            summed(0, L + 1)
            project(z, W96, wc[0][:, :], H)
            summed(1, L + 2)
            project(z, W96, wc[1][:, :], H)
            project(z, G, adp[1][:, :], G)
            turned(yq)
            gated(1, L + 3)
            summed(2, L + 4)
            project(z, H, w3[:, :], H)

        @block.vector
        def _(dve):
            do = Chain(dve, node_done)
            do(dve.memset(ring[:, 3200:3200 + 2 * SU * RW], 0.0))
            dve.memset(eps[:, :], 1e-5).then_inc(cols_ready, 1)
            dve.memset(half_pi[:, :], PI / 2).then_inc(cols_ready, 1)
            padv = pads[:, 0:PS_PAD * RW].rearrange("p (t c) -> p t c", c=RW)
            do(dve.memset(pads, 0.0))
            dve.memset(padv[:, :, C_KEY], PAD).then_inc(pads_ready, 1)
            dve.wait_ge(iota_ready, 1)
            do(dve.tensor_copy(ioc[:, :], ioi[:, 0:P]))
            do(dve.tensor_copy(iog, ioi[0:1, :]))

            def slots(key_i, rel, row, blk, n):
                do(dve.tensor_scalar(t1.bitcast(I32), key_i, 7, None, ALU.logical_shift_right))
                do(dve.tensor_copy(bf, t1.bitcast(I32)))
                do(dve.tensor_scalar(t1.bitcast(I32), key_i, P - 1, None, ALU.bitwise_and))
                do(dve.tensor_copy(rel, t1.bitcast(I32)))
                for c in range(NB):
                    do(dve.tensor_scalar(t1, bf, float(c), None, ALU.is_equal, ALU.add, accum_out=cnt[0:EP, c:c + 1]))
                dve.sem_inc(counts_ready, 1)
                dve.wait_ge(sums_ready, n + 1)
                do(dve.tensor_scalar(gi[:, :], ps_p[:, 0, 0:NB], float(GS - 1), None, ALU.add))
                do(dve.tensor_scalar(gi[:, :], gi[:, :], 8, None, ALU.logical_shift_right))
                do(dve.tensor_copy(gf[:, :], gi[:, :]))
                do(dve.tensor_tensor_scan(incl[:, :], gf[:, :], zero49[:, :], 0.0, ALU.add, ALU.add))
                do(dve.tensor_tensor(base[:, :], incl[:, :], gf[:, :], ALU.subtract))
                do(dve.tensor_scalar(base[:, :], base[:, :], float(GS), -1.0, ALU.mult, ALU.add))
                do(dve.tensor_tensor(base[0:EP, :], base[0:EP, :], ps_p[0:EP, 1, 0:NB], ALU.add))
                do(dve.memset(pos, 0.0))
                do(dve.memset(blf, 0.0))
                do.base = do.base + do.n
                do.n = 0
                b0 = do.base
                with dve.Fori(0, NB) as c:
                    do.base, do.n = c * 5 + b0, 0
                    col = bass.ds(c, 1)
                    do(dve.tensor_scalar(t1, bf, iocf[0:EP, col], None, ALU.is_equal))
                    do(dve.tensor_tensor_scan(t2, t1, zero_e, base[0:EP, col], ALU.add, ALU.add))
                    do(dve.tensor_tensor(t1, t1, t2, ALU.mult))
                    do(dve.tensor_tensor(pos, pos, t1, ALU.add))
                    do(dve.scalar_tensor_tensor(blf, iog, incl[0:1, col], blf, ALU.is_ge, ALU.add))
                do.base, do.n = b0 + NB * 5, 0
                do(dve.tensor_scalar(blk[:, :], blf, float(NB - 1), None, ALU.min))
                do(dve.tensor_copy(t1.bitcast(I32), pos))
                do(dve.tensor_scalar(t2.bitcast(I32), t1.bitcast(I32), P - 1, None, ALU.bitwise_and))
                do(dve.tensor_scalar(pos.bitcast(I32), t1.bitcast(I32), 7, None, ALU.logical_shift_right))
                do(dve.scalar_tensor_tensor(row, t2.bitcast(I32), float(NT), pos.bitcast(I32), ALU.mult, ALU.add))

            iocf = ioc
            zero49 = z1
            do(dve.memset(zero49[:, :], 0.0))
            do(dve.memset(zero_e, 0.0))
            dve.wait_ge(ints_loaded, 48)
            do(dve.tensor_copy(oth_e, dst_i))
            slots(src_i, krel_e, row_s, blk_s, 0)
            dve.sem_inc(rows_placed, 1)
            dve.wait_ge(pads_stored, 16 * (NT // PS_PAD))
            do(dve.memset(pads, 0.0))
            do(dve.memset(pads.rearrange("p (t c) -> p t c", c=2)[:, :, 1], PAD))
            dve.sem_inc(pairs_ready, 1)
            do(dve.tensor_copy(pair_e[:, :, 0], src_i))
            slots(dst_i, pair_e[:, :, 1], row_d, blk_d, 1)
            dve.sem_inc(pairs_placed, 1)
            for c in range(NT // XT):
                dve.wait_ge(chunk_loaded[c % 2], 16 * (c // 2 + 1))
                v = (z, yq)[c % 2][:, 0:XT * RW].rearrange("p (t c) -> p t c", c=RW)
                o = slice(c * XT, (c + 1) * XT)
                do(dve.tensor_copy(idx_s[:, o], v[:, :, C_IDX]))
                do(dve.tensor_copy(key_s[:, o], v[:, :, C_KEY]))
                do(dve.tensor_copy(cut_w[:, o], v[:, :, C_W]))
                dve.sem_inc(chunk_used, 1)
            do(dve.memset(idx_s[:, NT:NT + 2 * RING], 0))
            keep = acc[:, 0:NT]
            do(dve.tensor_scalar(keep, cut_w[:, :], CUT, 0.5, ALU.is_lt, ALU.mult))
            do(dve.tensor_scalar(yq[:, 0:NT], cut_w[:, :], -1.0, None, ALU.mult))
            do(dve.tensor_tensor(cut_w[:, :], cut_w[:, :], yq[:, 0:NT], ALU.max))
            do(dve.tensor_scalar(cut_w[:, :], cut_w[:, :], CUT, None, ALU.min))
            do(dve.memset(xs3[:, NB - 1, :], 0.0))
            dve.sem_inc(x_cleared, 1)
            dve.wait_ge(nodes_loaded, 64)
            do(dve.tensor_scalar(logm[:, :], mult[:, :], 1.0, None, ALU.max))
            dve.sem_inc(angle_ready, 1)
            do(dve.memset(z[:, :], 0.0))
            do(dve.memset(yq[:, :], 0.0))
            dve.wait_ge(cosine_done, 2)
            do(dve.scalar_tensor_tensor(cut_w[:, :], cut_w[:, :], 1.0, keep, ALU.add, ALU.mult))
            do(dve.memset(qt[:, :], 1.0))
            do(dve.memset(hid[0:H + 1, :], 1.0))

            class At:
                ln = proj = turn = 0

            def bc(v, w=NB):
                return v.unsqueeze(2).to_broadcast([P, w, H])

            def wide(v, w=H):
                return v.unsqueeze(1).to_broadcast([P, NB, w])

            def norm(src, dst, w=NB, relu=False):
                xc = tabs[:, 0:w * H].rearrange("p (b c) -> p b c", c=H)
                do(dve.tensor_reduce(ln_a[:, 0:w], src, AX.X, ALU.add))
                do(dve.tensor_scalar(ln_a[:, 0:w], ln_a[:, 0:w], 1.0 / H, None, ALU.mult))
                do(dve.tensor_tensor(xc, src, bc(ln_a[:, 0:w], w), ALU.subtract))
                do(dve.tensor_tensor(dst, xc, xc, ALU.mult))
                do(dve.tensor_reduce(ln_b[:, 0:w], dst, AX.X, ALU.add))
                dve.sem_inc(ln_var, 1)
                dve.wait_ge(ln_std, At.ln + 1)
                do(dve.reciprocal(ln_d[:, 0:w], ln_c[:, 0:w]))
                if relu:
                    do(dve.scalar_tensor_tensor(dst, xc, 0.0, bc(ln_d[:, 0:w], w), ALU.max, ALU.mult))
                else:
                    do(dve.tensor_tensor(dst, xc, bc(ln_d[:, 0:w], w), ALU.mult))
                At.ln = At.ln + 1

            def projected(n):
                b0 = At.proj * NB7
                with dve.Fori(0, NB7) as j:
                    hold(dve, "dve", (proj_mm, b0 + j + 1))
                    dve.tensor_copy(yq3[:, bass.ds(j * NB7, NB7), 0:n],
                                    ps[:, 4 * 512:4 * 512 + NB7 * P].rearrange("p (b c) -> p b c", c=P)[:, :, 0:n]).then_inc(proj_out, 1)
                At.proj = At.proj + 1
                dve.wait_ge(proj_out, b0 + NB7)

            def begin(idx):
                do(dve.memset(acc[:, :], 0.0))
                dve.tensor_copy(ids[:, :], idx[:, 0:RING * GT]).then_inc(idx_staged, 1)

            def add_up(sums, base, idx, blk, scale):
                def step(g, s):
                    b = dve.value_load(blk[0:1, bass.ds(g, 1)], min_val=0, max_val=NB - 1)
                    o = acc[:, bass.ds(b * TC, TC)]
                    dve.wait_ge(sums["agg"], base + g + 1)
                    again(dve, sums["acc"], base, g, 1)
                    if scale is None:
                        dve.tensor_tensor(o, o, ps_a[:, s % 2, 0:TC], ALU.add).then_inc(sums["acc"], 1)
                    else:
                        dve.wait_ge(sums["decay"], base + g + 1)
                        dve.scalar_tensor_tensor(o, o, scale[:, s:s + 1], ps_a[:, s % 2, 0:TC], ALU.mult, ALU.add).then_inc(sums["acc"], 1)
                    dve.tensor_copy(ids[:, s * GT:(s + 1) * GT], idx[:, bass.ds(g * GT + RING * GT, GT)]).then_inc(idx_staged, 1)
                return step

            def one_hot(key, g, s, dst, op):
                return dve.tensor_tensor(dst, ioc[:, :].unsqueeze(1).to_broadcast([P, GT, P]),
                                         key[:, bass.ds(g * GT, GT)].unsqueeze(2).to_broadcast([P, GT, P]), op)

            def gated(c, pass_no):
                base = c * NG

                def front(g, s):
                    one_hot(key_s, g, s, hot4[:, s], ALU.is_equal).then_inc(gate["hot"], 1)
                    dve.wait_ge(gathered[s], got(pass_no, g, s))
                    dve.tensor_tensor(hcut4[:, s], rows4[:, s, :, 0:H],
                                      cut_w[:, bass.ds(g * GT, GT)].unsqueeze(2).to_broadcast([P, GT, H]), ALU.mult).then_inc(gate["hcut"], 1)

                def logits(g, s):
                    dve.wait_ge(gate["bil"], base + g + 1)
                    dve.wait_ge(gate["hot"], base + g + 1)
                    for t in range(GT):
                        last = dve.tensor_tensor_reduce(out=junk[:, (s % 4) * GS + t * P:(s % 4) * GS + (t + 1) * P], in0=hot4[:, s, t, :], in1=ps_p[:, s % 2, t * P:(t + 1) * P],
                                                        scale=1.0, scalar=0.0, op0=ALU.mult, op1=ALU.add,
                                                        accum_out=logit[:, s * GT + t:s * GT + t + 1])
                    last.then_inc(gate["logit"], 1)

                def message(g, s):
                    dve.wait_ge(gate["out"], base + g + 1)
                    dve.wait_ge(gate["hcut"], base + g + 1)
                    dve.wait_ge(gate["logit"], base + g + 1)
                    for t in range(GT):
                        last = dve.scalar_tensor_tensor(msg4[:, s, t, 0:H], ps_a[:, s % 2, P + t * H:P + (t + 1) * H],
                                                        logit[:, s * GT + t:s * GT + t + 1], hcut4[:, s, t, :], ALU.add, ALU.mult)
                    last.then_inc(gate["msg"], 1)

                walk(dve, [(0, front), (2, logits), (4, message), (6, add_up(gate, base, idx_s, blk_s, None))], 6)
                dve.wait_ge(gate["acc"], base + NG)

            def attention(base, pass_no):
                def front(g, s):
                    r = s % 4
                    one_hot(key_s, g, s, nothot4[:, r], ALU.not_equal).then_inc(att["mask"], 1)
                    dve.wait_ge(gathered[s], got(pass_no, g, s))
                    dve.wait_ge(ea_loaded[s], got_ea(pass_no, g, s))
                    dve.scalar_tensor_tensor(rows4[:, s, :, 0:R], ear4[:, s, :, 0:R], 0.1, rows4[:, s, :, 0:R],
                                             ALU.mult, ALU.add).then_inc(att["keys"], 1)

                def peak(g, s):
                    b = dve.value_load(blk_s[0:1, bass.ds(g, 1)], min_val=0, max_val=NB - 1)
                    dve.wait_ge(att["scores"], base + g + 1)
                    dve.tensor_reduce(gmax[:, s:s + 1], ps_s[:, s % 2, 0:GS], AX.X, ALU.max, negate=True).then_inc(att["gmax"], 1)
                    dve.wait_ge(att["gmax"], base + g + 1)
                    again(dve, att["saved"], base, g, 1)
                    dve.tensor_tensor(nmn[:, s:s + 1], gmax[:, s:s + 1], nmax[:, bass.ds(b, 1)], ALU.min).then_inc(att["nmn"], 1)
                    dve.wait_ge(att["nmn"], base + g + 1)
                    dve.tensor_tensor(rdif[:, s:s + 1], nmn[:, s:s + 1], nmax[:, bass.ds(b, 1)], ALU.subtract).then_inc(att["rdif"], 1)
                    dve.wait_ge(att["rdif"], base + g + 1)
                    dve.tensor_tensor(nmax[:, bass.ds(b, 1)], gmax[:, s:s + 1], nmax[:, bass.ds(b, 1)], ALU.min).then_inc(att["saved"], 1)

                walk(dve, [(0, front), (1, peak), (5, add_up(att, base, idx_s, blk_s, decay))], 5)
                dve.wait_ge(att["acc"], base + NG)

            def summed(c):
                base = c * NG

                def front(g, s):
                    one_hot(key_d, g, s, hot4[:, s], ALU.is_equal).then_inc(conv["hot"], 1)

                walk(dve, [(0, front), (2, add_up(conv, base, idx_d, blk_d, None))], 2)
                dve.wait_ge(conv["acc"], base + NG)

            def gated_table():
                tg = blocks(tabs, TG)
                do(dve.tensor_copy(z3[:, :, 0:G], emb3))
                dve.sem_inc(x_ready, 1)
                projected(G)
                dve.sem_inc(x_ready, 1)
                dve.wait_ge(turn_evac, At.turn)
                norm(xs3, z3[:, :, 0:H], relu=True)
                do(dve.tensor_tensor(tg[:, :, 0:H], z3[:, :, 0:H], bc(mult[:, :]), ALU.mult))
                do(dve.tensor_copy(tg[:, :, H], mult[:, :]))
                do(dve.tensor_copy(tg[:, :, H + 1:TG], emb3))
                dve.sem_inc(table_ready, 1)
                begin(idx_s)

            def gated_end(gain, shift):
                do(dve.tensor_scalar(ln_a[:, 0:NB], acc3[:, :, H], 1e-8, None, ALU.max))
                do(dve.reciprocal(ln_a[:, 0:NB], ln_a[:, 0:NB]))
                do(dve.tensor_tensor(yq3[:, :, 0:H], acc3[:, :, 0:H], bc(ln_a[:, 0:NB]), ALU.mult))
                do(dve.tensor_tensor(yq3[:, :, 0:H], yq3[:, :, 0:H], z3[:, :, 0:H], ALU.add))
                norm(yq3[:, :, 0:H], z3[:, :, 0:H])
                do(dve.tensor_tensor(z3[:, :, 0:H], z3[:, :, 0:H], wide(gain), ALU.mult))
                do(dve.tensor_tensor(z3[:, :, 0:H], z3[:, :, 0:H], wide(shift), ALU.add))

            def conv_table():
                tc = blocks(tabs, TC)
                do(dve.tensor_copy(tc[:, :, 0:H], z3[:, :, 0:H]))
                do(dve.memset(tc[:, :, H], 1.0))
                dve.sem_inc(table_ready, 1)
                begin(idx_d)

            dve.wait_ge(params_loaded, PARAMS * 16)
            dve.wait_ge(wmu_moved, 16)
            dve.wait_ge(nodes_loaded, 96)
            dve.wait_ge(emb_gathered, 16 * NB)
            At.turn = NB7
            gated_table()
            gated(0, 0)
            dve.sem_inc(emb_used, 1)
            gated_end(vec["gn"][:, :], vec["bn"][:, :])
            ta = blocks(tabs, TA)
            b0 = do.base + do.n
            p0, n0 = At.proj, At.ln
            with dve.Fori(0, L) as l:
                do.base, do.n = l * LAYER_CHAIN + b0, 0
                At.proj, At.ln = l * LAYER_PROJ + p0, l * LAYER_LN + n0
                for cur, every, w in ((lcur, lpar, 6 * H), (wqk_c, wqk, W96), (ww_c, ww, H)):
                    dve.tensor_copy(cur[:, :], every[:, bass.ds(l * w, w)]).then_inc(node_done, 1)
                do.n = 3
                dve.wait_ge(node_done, do.base + 3)
                dve.sem_inc(x_ready, 1)
                projected(W96)
                qk = yq[:, :].rearrange("p (b c) -> p b c", c=H)
                norm(qk, qk, 2 * NB)
                do(dve.tensor_tensor(yq3, yq3, wide(lcur[:, 0:W96], W96), ALU.mult))
                do(dve.tensor_tensor(yq3[:, :, 0:H], yq3[:, :, 0:H], wide(lcur[:, W96:3 * H]), ALU.add))
                dve.sem_inc(x_ready, 1)
                do(dve.tensor_tensor(ta[:, :, 0:H], yq3[:, :, H:W96], wide(lcur[:, 3 * H:4 * H]), ALU.add))
                do(dve.tensor_copy(ta[:, :, H], logm[:, :]))
                do(dve.tensor_copy(ta[:, :, H + 1:TA - 1], z3[:, :, 0:H]))
                do(dve.memset(ta[:, :, TA - 1], 1.0))
                dve.sem_inc(table_ready, 1)
                do(dve.memset(nmax[:, :], 1e20))
                begin(idx_s)
                attention(l * NG, l + 1)
                do(dve.tensor_scalar(ln_a[:, 0:NB], acc3[:, :, H], 1e-10, None, ALU.add))
                do(dve.reciprocal(ln_a[:, 0:NB], ln_a[:, 0:NB]))
                do(dve.tensor_tensor(z3[:, :, H:W96], acc3[:, :, 0:H], bc(ln_a[:, 0:NB]), ALU.mult))
                dve.sem_inc(x_ready, 1)
                projected(H)
                do(dve.scalar_tensor_tensor(yq3[:, :, 0:H], yq3[:, :, 0:H], 0.01, yq3[:, :, 0:H], ALU.mult, ALU.max))
                do(dve.tensor_tensor(yq3[:, :, 0:H], yq3[:, :, 0:H], z3[:, :, 0:H], ALU.add))
                norm(yq3[:, :, 0:H], z3[:, :, 0:H])
                do(dve.tensor_tensor(z3[:, :, 0:H], z3[:, :, 0:H], wide(lcur[:, 4 * H:5 * H]), ALU.mult))
                do(dve.tensor_tensor(z3[:, :, 0:H], z3[:, :, 0:H], wide(lcur[:, 5 * H:6 * H]), ALU.add))
                dve.sem_inc(tick["dve"], 1)
                assert do.n == LAYER_CHAIN, do.n
            do.base, do.n = b0 + L * LAYER_CHAIN, 0
            At.proj, At.ln = L * LAYER_PROJ + p0, L * LAYER_LN + n0
            do(dve.tensor_tensor(xs3, xs3, z3[:, :, 0:H], ALU.add))
            norm(xs3, z3[:, :, 0:H], relu=True)
            dve.sem_inc(tabs_free, 1)
            dve.wait_ge(pairs_loaded, 16)
            do(dve.tensor_copy(idx_d[:, 0:NT], pair_l[:, :, 0]))
            do(dve.tensor_copy(key_d[:, :], pair_l[:, :, 1]))
            do(dve.memset(idx_d[:, NT:NT + 2 * RING], 0))
            conv_table()
            summed(0)
            do(dve.tensor_scalar(deg[:, :], acc3[:, :, H], 1.0, None, ALU.add))
            do(dve.tensor_copy(z3[:, :, H:W96], acc3[:, :, 0:H]))
            dve.sem_inc(x_ready, 1)
            projected(H)
            do(dve.tensor_tensor(yq3[:, :, 0:H], yq3[:, :, 0:H], wide(vec["b1"][:, :]), ALU.add))
            do(dve.tensor_scalar(z3[:, :, 0:H], yq3[:, :, 0:H], 0.0, None, ALU.max))
            conv_table()
            summed(1)
            do(dve.tensor_copy(z3[:, :, H:W96], acc3[:, :, 0:H]))
            dve.sem_inc(x_ready, 1)
            projected(H)
            do(dve.tensor_tensor(yq3[:, :, 0:H], yq3[:, :, 0:H], wide(vec["b2"][:, :]), ALU.add))
            do(dve.tensor_tensor(xs3, xs3, yq3[:, :, 0:H], ALU.add))
            dve.wait_ge(emb_gathered, 32 * NB)
            At.turn = (L + 2) * NB7
            gated_table()
            gated(1, L + 3)
            gated_end(vec["gamma"][:, :], vec["beta"][:, :])
            do(dve.tensor_tensor(xs3, xs3, z3[:, :, 0:H], ALU.add))
            norm(xs3, z3[:, :, 0:H], relu=True)
            dve.sem_inc(degree_ready, 1)
            dve.wait_ge(degree_root, 1)
            do(dve.reciprocal(ln_d[:, 0:NB], deg[:, :]))
            do(dve.tensor_tensor(z3[:, :, 0:H], z3[:, :, 0:H], bc(ln_d[:, 0:NB]), ALU.mult))
            conv_table()
            summed(2)
            do(dve.tensor_tensor(z3[:, :, 0:H], z3[:, :, 0:H], acc3[:, :, 0:H], ALU.add))
            do(dve.tensor_tensor(z3[:, :, 0:H], z3[:, :, 0:H], bc(ln_d[:, 0:NB]), ALU.mult))
            dve.sem_inc(x_ready, 1)
            projected(H)
            do(dve.tensor_tensor(yq3[:, :, 0:H], yq3[:, :, 0:H], wide(vec["b3"][:, :]), ALU.add))
            do(dve.tensor_tensor(xs3, xs3, yq3[:, :, 0:H], ALU.add))
            dve.sem_inc(x_ready, 1)


_INS = ["x", "src", "dst", "edge_attr_40", "edge_weight", "node_type_119", "node_vec",
        "L0_gnn_Wq", "L0_gnn_gq", "L0_gnn_bq", "L0_gnn_Wk", "L0_gnn_gk", "L0_gnn_bk", "L0_gnn_Wu", "L0_gnn_go",
        "L0_gnn_bo", "L0_gnn_F1W", "L0_gnn_F1b", "L0_gnn_F2W", "L0_gnn_F2b", "L0_gnn_gn", "L0_gnn_bn", "L0_gnn_emb",
        "L1_gnn_w_rel1", "L1_gnn_w_root1", "L1_gnn_b1", "L1_gnn_w_rel2", "L1_gnn_w_root2", "L1_gnn_b2",
        "L2_gnn_b1", "L2_gnn_b2", "L2_gnn_emb", "L2_gnn_adaptW", "L2_gnn_gamma", "L2_gnn_beta", "L3_gnn_W", "L3_gnn_b"]
_TURNED = {"Wm_t": ("L0_gnn_Wm", (0, 2, 1)), "adapt_t": ("L0_gnn_adapt", (1, 0)),
           "W1_t": ("L2_gnn_W1", (1, 0)), "W2_t": ("L2_gnn_W2", (1, 0))}


def kernel(**inputs):
    import numpy as np
    import concourse.bacc as bacc
    from concourse.bass_utils import run_bass_kernel_spmd

    nc = bacc.Bacc("TRN2", target_bir_lowering=False, num_devices=1)
    laid = {n: np.ascontiguousarray(inputs[n]) for n in _INS}
    for n, (source, order) in _TURNED.items():
        laid[n] = np.ascontiguousarray(np.transpose(np.asarray(inputs[source]), order))
    aps = {n: nc.dram_tensor("in_" + n, v.shape, mybir.dt.from_np(v.dtype), kind="ExternalInput").ap()
           for n, v in laid.items()}
    out = nc.dram_tensor("out_0", (N, H), F32, kind="ExternalOutput").ap()
    build(nc, aps, out)
    r = run_bass_kernel_spmd(nc, [{"in_" + n: v for n, v in laid.items()}], core_ids=[0])
    return r.results[0]["out_0"]
```

```python
from contextlib import ExitStack

import concourse.bass as bass
from concourse import mybir

F32 = mybir.dt.float32
BF16 = mybir.dt.bfloat16
I32 = mybir.dt.int32
ALU = mybir.AluOpType
ACT = mybir.ActivationFunctionType
AX = mybir.AxisListType
ACT_ENGINE, PE_ENGINE, DVE_ENGINE = (mybir.EngineType.Activation, mybir.EngineType.PE, mybir.EngineType.DVE)

P = 128
N = 6250
E = 200000
H = 48
R = 40
G = 32
L = 4
CUT = 6.0
PI = 3.141592653589793

NB = -(-N // P)
LAST = N - (NB - 1) * P
GT = 2
GS = GT * P
RING = 16
R8 = 8
NG = -(-((E + NB * (GS - 1)) // GS) // RING) * RING
NT = NG * GT
PAD = 255.0

EP, ET = 125, E // 125
SU = 8
SI = ET // (2 * SU)
SU2 = 16
SI2 = ET // (2 * SU2)
SI2_EARLY = 8
PACK = 256
RW = 44
C_W, C_KEY, C_IDX = R, R + 1, R + 2
XT = 104
TG, TA, TC = H + 1 + G, 2 * H + 2, H + 1
BIG = 1.0e30
NB7 = 7
W96 = 2 * H
PS_PAD = 64

TURN, BACK = 1, 5
LAYER_CHAIN = 32
PARAMS = 7 + 6 + 2 + 3 + 2 * 7 + 1
LAST_X = 2 + 3 * L + 1 + 1 + 2 + 1 + 1
LAYER_PROJ, LAYER_TURN, LAYER_LN, LAYER_X = 2, 1, 2, 3

assert (BACK - TURN) % 2 == 0 and NB == NB7 * NB7 and ET * EP == E and SI * 2 * SU == ET and SI2 * 2 * SU2 == ET and N * PACK < 1 << 24 and NT % XT == 0 and NT % PS_PAD == 0


class Chain:

    def __init__(self, eng, sem):
        self.eng, self.sem, self.base, self.n = eng, sem, 0, 0

    def __call__(self, ins):
        self.n += 1
        ins.then_inc(self.sem, 1)
        self.eng.wait_ge(self.sem, self.base + self.n)


def again(eng, sem, base, g, ring):
    if isinstance(g, int) and g < ring:
        return
    eng.wait_ge(sem, base + g + 1 - ring)


def walk(eng, steps, blocks=None, also=None):
    depth = max(lag for lag, _ in steps)

    def load(first, count):
        if blocks is None:
            return {}
        nc, kind, row = blocks
        _, regs = nc.values_load_multi_w_load_instructions(
            row[0:1, bass.ds(first, count)], engines=(kind,), min_val=0, max_val=NB - 1,
            skip_runtime_bounds_check_because="VectorE clamps it")
        return regs

    def turn(k, u, regs, at):
        for lag, f in steps:
            if not isinstance(k, int) or 0 <= k - lag < NG:
                b = () if blocks is None else (regs[u - lag + at],)
                f(k - lag, (u - lag) % RING, *b)

    regs = load(0, RING)
    for u in range(RING):
        turn(u, u, regs, 0)
        if also:
            also(0, u)
    first = 1
    if also:
        first = SI2 - SI2_EARLY
        with eng.Fori(1, first) as i:
            for u in range(RING):
                turn(i * RING + u, u, {}, 0)
                also(i, u)
    with eng.Fori(first, NG // RING) as i:
        regs = load(i * RING - R8, RING + R8)
        for u in range(RING):
            turn(i * RING + u, u, regs, R8)
    if depth:
        regs = load(NG - R8, R8)
        for u in range(depth):
            turn(NG + u, u, regs, R8)


def build(nc, a, out):
    ctx = ExitStack()
    with ctx:
        def sb(name, shape, dt=F32):
            return ctx.enter_context(nc.sbuf_tensor(name, shape, dt))

        def sem(name):
            return ctx.enter_context(nc.semaphore(name))

        def dram(name, shape, dt=F32):
            return nc.dram_tensor(name, shape, dt, kind="Internal").ap()

        rec = dram("slot_records", [P, NT * RW])
        rec2 = dram("slot_pairs", [P, NT])
        gate1 = dram("gates_second", [P, NT * H])
        tab_g = dram("tab_gated", [NB * P, TG])
        tab_a = dram("tab_attention", [NB * P, TA])
        tab_c = dram("tab_conv", [NB * P, TC])
        rec_rows = rec.rearrange("p (t c) -> (p t) c", c=RW)
        rec2_rows = rec2.rearrange("p (t c) -> (p t) c", c=1)

        xs = sb("x_sum", [P, NB * H])
        z = sb("z", [P, NB * W96])
        yq = sb("yq", [P, NB * W96])
        tabs = sb("table_stage", [P, NB * TA])
        acc = sb("acc", [P, NB * TC])
        qt = sb("q_turned", [P, NB * P])
        emb = sb("emb_nodes", [P, NB * G])
        mult = sb("mult", [P, NB])
        logm = sb("log_mult", [P, NB])
        ztype = sb("node_type", [P, NB], I32)
        nmax = sb("neg_max", [P, NB])
        deg = sb("degree", [P, NB])
        ln_a, ln_b, ln_c, ln_d = (sb(f"ln_{c}", [P, 2 * NB]) for c in "abcd")
        idx_s = sb("idx_by_src", [P, NT + 2 * RING], I32)
        idx_d = sb("idx_by_dst", [P, NT + 2 * RING], I32)
        key_s = sb("key_by_src", [P, NT])
        cut_w = sb("cutoff", [P, NT])
        key_d = sb("key_by_dst", [P, NT])
        blk_s = sb("block_by_src", [1, NG], I32)
        blk_d = sb("block_by_dst", [1, NG], I32)
        rows = sb("gathered", [P, RING * GT * TA])
        ear = sb("edge_records", [P, R8 * GT * H])
        kept = sb("gates_kept", [P, 4 * GT * H])
        ids = sb("idx_stage", [P, RING * GT], I32)
        ring = sb("ring", [P, 7200])
        hot = ring[:, 0:R8 * GS]
        nothot = ring[:, 0:4 * P].bitcast(BF16)
        prob = ring[:, 512:512 + 4 * GS]
        probt = ring[:, 1536:1536 + 4 * GS]
        kturn = ring[:, 2560:2560 + 4 * GS]
        qcur = ring[:, 3584:3584 + 4 * P]
        gmax = ring[:, 4096:4096 + R8]
        nmn = ring[:, 4104:4104 + R8]
        rdif = ring[:, 4112:4112 + R8]
        decay = ring[:, 4120:4120 + R8]
        hcut = ring[:, 2048:2048 + R8 * GT * H]
        msg = ring[:, 2816:2816 + R8 * GT * TC]
        eat = ring[:, 3600:3600 + 4 * GS]
        ebt = ring[:, 4624:4624 + 4 * GS]
        hid = ring[:, 5648:5648 + 4 * GS]
        logit = ring[:, 6672:6672 + R8 * GT]
        junk = ring[:, 6688:6688 + 2 * GS].bitcast(BF16)
        xt_sb = ring[:, 4624:4624 + NB7 * P]
        pads = qt[:, ET:ET + PS_PAD * RW]
        pair_l = tabs[:, 0:NT]
        stage = ring[:, 3200:3200 + 2 * SU * RW].rearrange("p (u j c) -> p u j c", u=2, c=RW)
        stage_i = ring[:, 3904:3904 + 2 * SU].bitcast(I32).rearrange("p (u j) -> p u j", u=2)
        pair_e = key_d[0:EP, 0:ET]
        stage2 = sb("pair_stage", [P, 2, SU2])
        stage2_i = sb("pair_row_stage", [P, 2, SU2], I32)
        w_e = qt[0:EP, 0:ET]
        krel_e = tabs[0:EP, 0:ET]
        oth_e = tabs[0:EP, ET:2 * ET]
        src_i = acc[0:EP, 0:ET].bitcast(I32)
        dst_i = tabs[0:EP, 2 * ET:3 * ET].bitcast(I32)
        row_s = xs[0:EP, 0:ET].bitcast(I32)
        row_d = idx_d[0:EP, 0:ET]
        bf, t1 = z[0:EP, 0:ET], z[0:EP, ET:2 * ET]
        t2, pos = yq[0:EP, 0:ET], yq[0:EP, ET:2 * ET]
        zero_e = cut_w[0:EP, 0:ET]
        cnt = sb("cnt", [P, NB])
        gf, incl, base = sb("gf", [P, NB]), sb("incl", [P, NB]), sb("base", [P, NB])
        gi = sb("gi", [P, NB], I32)
        iog, blf = z[0:1, 2 * ET:2 * ET + NG], yq[0:1, 2 * ET:2 * ET + NG]
        ioi = ring[:, 4000:4000 + NG].bitcast(I32)
        z1 = sb("zero_blocks", [P, NB])
        ident = sb("ident", [P, P])
        tri = sb("tri", [P, P])
        ones = sb("ones", [P, P])
        ioc = sb("iota_col", [P, P])
        neg_i = sb("neg_ident", [P, P], BF16)
        eps = sb("eps", [P, 1])
        half_pi = sb("half_pi", [P, 1])
        vec = {n: sb("v_" + n, [P, H]) for n in ("gn", "bn", "gamma", "beta", "b1", "b2", "b3")}
        lpar = sb("layer_vec", [P, L * 6 * H])
        lcur = sb("layer_cur", [P, 6 * H])
        wqk = sb("wqk", [H, L * W96])
        wqk_c = sb("wqk_c", [H, W96])
        ww = sb("ww", [W96, L * H])
        ww_c = sb("ww_c", [W96, H])
        wm_t, wub, wmu = (ring[0:H, 4900 + k * L * H:4900 + (k + 1) * L * H] for k in range(3))
        f1 = sb("f1", [R, W96])
        fb1 = sb("fb1", [W96, 1])
        f2 = sb("f2", [W96 + 1, W96])
        adp = [sb(f"adp_{k}", [G, G]) for k in range(2)]
        wc = [sb(f"wc_{k}", [W96, H]) for k in range(2)]
        w3 = sb("w3", [H, H])

        def blocks(t, w):
            return t[:, 0:NB * w].rearrange("p (b c) -> p b c", c=w)

        def ringv(t, n, w):
            return t.rearrange("p (s t c) -> p s t c", s=n, c=w)

        xs3, z3, yq3 = blocks(xs, H), blocks(z, W96), blocks(yq, W96)
        acc3, emb3 = blocks(acc, TC), blocks(emb, G)
        rows4 = ringv(rows[:, :], RING, TA)
        ear4 = ringv(ear[:, 0:R8 * GT * RW], R8, RW)
        gear4 = ringv(ear[:, :], R8, H)
        kept4 = kept[:, :].rearrange("p (s c) -> p s c", s=4)
        hot4, nothot4 = ringv(hot, R8, P), ringv(nothot, 4, P)
        hcut4, msg4 = ringv(hcut, R8, H), ringv(msg, R8, TC)

        ps = ctx.enter_context(nc.psum_tensor("ps", [P, 8 * 512], F32))
        psv = ps[:, :].rearrange("p (k n) -> p k n", n=512)
        ps_t, ps_s, ps_p, ps_a = (psv[:, 2 * k:2 * k + 2, :] for k in range(4))
        ps_q = psv[:, 2:6, :]

        tick = {e: sem(f"tick_{e}") for e in ("pool", "act", "pe", "dve")}
        f2_cleared = sem("f2_cleared")
        pads_ready, pads_stored, pairs_ready, pairs_stored = (sem(s) for s in (
            "pads_ready", "pads_stored", "pairs_ready", "pairs_stored"))
        ints_loaded, params_loaded, nodes_loaded, nodes_zeroed = (sem(s) for s in (
            "ints_loaded", "params_loaded", "nodes_loaded", "nodes_zeroed"))
        consts_ready, iota_ready, cols_ready = sem("consts_ready"), sem("iota_ready"), sem("cols_ready")
        counts_ready, sums_ready = sem("counts_ready"), sem("sums_ready")
        rows_placed, pairs_placed = sem("rows_placed"), sem("pairs_placed")
        rec_loaded = [sem(f"rec_loaded{u}") for u in range(2)]
        rec_staged = sem("rec_staged")
        scattered = [sem(f"scattered{u}") for u in range(2)]
        pair_staged = [sem(f"pair_staged{u}") for u in range(2)]
        pair_scattered = [sem(f"pair_scattered{u}") for u in range(2)]
        chunk_loaded = [sem(f"chunk_loaded{u}") for u in range(2)]
        chunk_used = sem("chunk_used")
        pairs_loaded = sem("pairs_loaded")
        emb_gathered = sem("emb_gathered")
        emb_used = sem("emb_used")
        wmu_made, wmu_copied, wmu_moved = sem("wmu_made"), sem("wmu_copied"), sem("wmu_moved")
        node_done = sem("node_done")
        ln_var, ln_std = sem("ln_var"), sem("ln_std")
        rec_parts, x_cleared, tabs_free = sem("rec_parts"), sem("x_cleared"), sem("tabs_free")
        angle_ready, cosine_done, degree_ready, degree_root = (sem(s) for s in (
            "angle_ready", "cosine_done", "degree_ready", "degree_root"))
        x_ready = sem("x_ready")
        proj_t, proj_evac, proj_mm, proj_out = (sem(s) for s in ("proj_t", "proj_evac", "proj_mm", "proj_out"))
        turn_t, turn_evac = sem("turn_t"), sem("turn_evac")
        table_ready, table_stored = sem("table_ready"), sem("table_stored")
        idx_staged = sem("idx_staged")
        gathered = [sem(f"gathered{s}") for s in range(RING)]
        ea_loaded = [sem(f"ea_loaded{s}") for s in range(R8)]
        conv = {n: sem("conv_" + n) for n in ("hot", "agg", "acc")}
        gate = {n: sem("gate_" + n) for n in (
            "hot", "hcut", "t", "evac", "evac_e", "mj", "hid", "bil", "act", "logit", "out", "msg", "agg", "acc", "kept")}
        gates_stored = [sem(f"gates_stored{s}") for s in range(4)]
        att = {n: sem("att_" + n) for n in (
            "keys", "mask", "kt", "kt_evac", "q", "scores", "gmax", "nmn", "rdif", "saved",
            "decay", "probs", "pt", "pt_evac", "agg", "acc")}
        out_stored = sem("out_stored")

        def hold(eng, name, *waits):
            for s, v in waits:
                eng.wait_ge(s, v)
                eng.sem_inc(tick[name], 1)

        block = ctx.enter_context(nc.Block())

        @block.sync
        def _(sp):
            sp.dma_start(src_i, a["src"].rearrange("(p t) -> p t", p=EP)).then_inc(ints_loaded, 16)
            sp.dma_start(dst_i, a["dst"].rearrange("(p t) -> p t", p=EP)).then_inc(ints_loaded, 16)
            sp.dma_start(w_e, a["edge_weight"].rearrange("(p t) -> p t", p=EP)).then_inc(ints_loaded, 16)

            sp.wait_ge(f2_cleared, 1)

            def par(dst, src):
                sp.dma_start(dst, src).then_inc(params_loaded, 16)

            for n, k in (("gn", "L0_gnn_gn"), ("bn", "L0_gnn_bn"), ("gamma", "L2_gnn_gamma"), ("beta", "L2_gnn_beta"),
                         ("b1", "L1_gnn_b1"), ("b2", "L1_gnn_b2"), ("b3", "L3_gnn_b")):
                par(vec[n][:, :], a[k].partition_broadcast(P))
            lp = lpar[:, :].rearrange("p (l k c) -> p l k c", l=L, c=H)
            for j, k in enumerate(("gq", "gk", "bq", "bk", "go", "bo")):
                par(lp[:, :, j, :], a["L0_gnn_" + k].partition_broadcast(P))
            wq3 = wqk[:, :].rearrange("p (l c) -> p l c", l=L)
            par(wq3[:, :, 0:H], a["L0_gnn_Wq"].rearrange("l k c -> k l c"))
            par(wq3[:, :, H:W96], a["L0_gnn_Wk"].rearrange("l k c -> k l c"))
            par(ww[0:H, :].rearrange("p (l c) -> p l c", l=L), a["L0_gnn_Wu"][:, 0:H, :].rearrange("l k c -> k l c"))
            par(wub.rearrange("p (l c) -> p l c", l=L), a["L0_gnn_Wu"][:, H:W96, :].rearrange("l k c -> k l c"))
            par(wm_t.rearrange("p (l c) -> p l c", l=L), a["Wm_t"].rearrange("l k c -> k l c"))
            for k, (w1, b1, w2, b2, ad) in enumerate((
                    ("L0_gnn_F1W", "L0_gnn_F1b", "L0_gnn_F2W", "L0_gnn_F2b", "adapt_t"),
                    ("W1_t", "L2_gnn_b1", "W2_t", "L2_gnn_b2", "L2_gnn_adaptW"))):
                o = slice(k * H, (k + 1) * H)
                par(f1[:, o], a[w1])
                par(fb1[o, :], a[b1].rearrange("(c k) -> c k", k=1))
                par(f2[o, o], a[w2])
                par(f2[W96:W96 + 1, o], a[b2].rearrange("(k c) -> k c", k=1))
                par(adp[k][:, :], a[ad])
                par(wc[k][0:H, :], a[f"L1_gnn_w_root{k + 1}"])
                par(wc[k][H:W96, :], a[f"L1_gnn_w_rel{k + 1}"])
            par(w3[:, :], a["L3_gnn_W"])
            sp.wait_ge(nodes_zeroed, 2)
            for dst, src in ((mult, a["node_vec"]), (ztype, a["node_type_119"])):
                sp.dma_start(dst[:, 0:NB - 1], src[0:(NB - 1) * P].rearrange("(b p) -> p b", p=P), allow_slow_non_contiguous=True).then_inc(nodes_loaded, 16)
                sp.dma_start(dst[0:LAST, NB - 1:NB], src[(NB - 1) * P:N].rearrange("(p k) -> p k", k=1)).then_inc(nodes_loaded, 16)
            sp.wait_ge(pads_ready, 1)
            for c in range(NT // PS_PAD):
                sp.dma_start(rec[:, c * PS_PAD * RW:(c + 1) * PS_PAD * RW], pads[:, 0:PS_PAD * RW]).then_inc(pads_stored, 16)
            sp.wait_ge(pairs_ready, 1)
            sp.dma_start(rec2, pads[:, 0:NT]).then_inc(pairs_stored, 16)
            sp.wait_ge(wmu_copied, 1)
            sp.dma_start(ww[H:W96, :], wmu).then_inc(wmu_moved, 16)

            ea = a["edge_attr_40"].rearrange("(p t) c -> p t c", p=EP)

            def load_ea(i, u):
                if not (isinstance(i, int) and i == 0):
                    sp.wait_ge(scattered[u], i * (16 * SU))
                sp.dma_start(stage[0:EP, u, :, 0:R], ea[:, bass.ds(i * (2 * SU) + u * SU, SU), :]).then_inc(rec_loaded[u], 16)

            sp.wait_ge(node_done, 1)
            for u in range(2):
                load_ea(0, u)
            with sp.Fori(1, SI) as i:
                for u in range(2):
                    load_ea(i, u)
            def load_pairs(i, u):
                if not (isinstance(i, int) and i == 0):
                    sp.wait_ge(pair_scattered[u], i * (16 * SU2))
                cols = bass.ds(i * (2 * SU2) + u * SU2, SU2)
                sp.dma_start(stage2_i[0:EP, u, :], row_d[:, cols]).then_inc(pair_staged[u], 16)
                sp.dma_start(stage2[0:EP, u, :], pair_e[:, cols]).then_inc(pair_staged[u], 16)

            sp.wait_ge(pairs_placed, 1)
            for u in range(2):
                load_pairs(0, u)
            for u in range(2):
                sp.wait_ge(scattered[u], SI * SU * 16)
            for c in range(NT // XT):
                if c >= 2:
                    sp.wait_ge(chunk_used, c - 1)
                sp.dma_start((z, yq)[c % 2][:, 0:XT * RW], rec[:, c * XT * RW:(c + 1) * XT * RW]).then_inc(chunk_loaded[c % 2], 16)
            with sp.Fori(1, SI2_EARLY) as i:
                for u in range(2):
                    load_pairs(i, u)
            sp.wait_ge(x_cleared, 1)
            sp.dma_start(xs3[:, 0:NB - 1, :], a["x"][0:(NB - 1) * P, :].rearrange("(b p) c -> p b c", p=P)).then_inc(nodes_loaded, 16)
            sp.dma_start(xs3[0:LAST, NB - 1, :], a["x"][(NB - 1) * P:N, :]).then_inc(nodes_loaded, 16)

            def store_table(tab, w, n):
                sp.wait_ge(table_ready, n)
                sp.dma_start(tab.rearrange("(b p) c -> p b c", p=P), blocks(tabs, w)).then_inc(table_stored, 16)

            def load_edges(base, used, store=(), also=None):
                def step(g, s):
                    s = s % R8
                    again(sp, used, base, g, R8)
                    sp.dma_start(ear[:, s * GT * RW:(s + 1) * GT * RW],
                                 rec[:, bass.ds(g * (GT * RW), GT * RW)]).then_inc(ea_loaded[s], 16)
                walk(sp, [(0, step), *store], also=also)

            def load_later_pairs(i, k):
                if k % R8 == 0:
                    load_pairs(i + SI2_EARLY, k // R8)

            def store_gates(g, s):
                sp.wait_ge(gate["kept"], g + 1)
                sp.dma_start(gate1[:, bass.ds(g * (GT * H), GT * H)], kept4[:, s % 4, :]).then_inc(gates_stored[s % 4], 16)

            def load_gates():
                def step(g, s):
                    s = s % R8
                    again(sp, gate["msg"], NG, g, R8)
                    sp.dma_start(ear[:, s * GT * H:(s + 1) * GT * H],
                                 gate1[:, bass.ds(g * (GT * H), GT * H)]).then_inc(ea_loaded[s], 16)
                walk(sp, [(0, step)])

            store_table(tab_g, TG, 1)
            load_edges(0, gate["t"], [(12, store_gates)], load_later_pairs)
            with sp.Fori(0, L) as l:
                store_table(tab_a, TA, l + 2)
                load_edges(l * NG, att["keys"])
            sp.wait_ge(tabs_free, 1)
            for u in range(2):
                sp.wait_ge(pair_scattered[u], SI2 * SU2 * 16)
            sp.dma_start(pair_l, rec2).then_inc(pairs_loaded, 16)
            store_table(tab_c, TC, L + 2)
            store_table(tab_c, TC, L + 3)
            store_table(tab_g, TG, L + 4)
            for k in range(4):
                sp.wait_ge(gates_stored[k], NG // 4 * 16)
            load_gates()
            store_table(tab_c, TC, L + 5)
            sp.wait_ge(x_ready, LAST_X)
            sp.dma_start(out[0:(NB - 1) * P, :].rearrange("(b p) c -> p b c", p=P), xs3[:, 0:NB - 1, :]).then_inc(out_stored, 16)
            sp.dma_start(out[(NB - 1) * P:N, :], xs3[0:LAST, NB - 1, :]).then_inc(out_stored, 16)
            sp.wait_ge(out_stored, 32)

        @block.gpsimd
        def _(pool):
            pool.iota(ioi, pattern=[[1, NG]], base=0, channel_multiplier=0).then_inc(iota_ready, 1)
            pool.memset(ones[:, :], 1.0).then_inc(consts_ready, 1)
            pool.memset(ident[:, :], 0.0).then_inc(consts_ready, 1)
            pool.memset(neg_i[:, :], 0.0).then_inc(consts_ready, 1)
            pool.memset(tri[:, :], 1.0).then_inc(consts_ready, 1)
            pool.memset(mult[:, :], 1.0).then_inc(nodes_zeroed, 1)
            pool.memset(ztype[:, :], 0).then_inc(nodes_zeroed, 1)
            pool.wait_ge(consts_ready, 4)
            pool.affine_select(out=ident[:, :], in_=ident[:, :], compare_op=ALU.not_equal, fill=1.0, base=0,
                               pattern=[[-1, P]], channel_multiplier=1).then_inc(consts_ready, 1)
            pool.affine_select(out=neg_i[:, :], in_=neg_i[:, :], compare_op=ALU.not_equal, fill=-BIG, base=0,
                               pattern=[[-1, P]], channel_multiplier=1).then_inc(consts_ready, 1)
            pool.affine_select(out=tri[:, :], in_=tri[:, :], compare_op=ALU.is_gt, fill=0.0, base=0,
                               pattern=[[1, P]], channel_multiplier=-1).then_inc(consts_ready, 1)

            def gather_emb(table):
                for b in range(NB):
                    pool.indirect_dma_start(out=emb3[:, b, :], out_offset=None, in_=table,
                                            in_offset=bass.IndirectOffsetOnAxis(ap=ztype[:, b:b + 1], axis=0)).then_inc(emb_gathered, 16)

            pool.wait_ge(nodes_loaded, 64)
            gather_emb(a["L0_gnn_emb"])

            def scatter(i, u):
                hold(pool, "pool", (rec_loaded[u], (i + 1) * 16), (rec_staged, i * 2 + u + 1))
                for j in range(SU):
                    pool.indirect_dma_start(out=rec_rows, out_offset=bass.IndirectOffsetOnAxis(ap=stage_i[0:EP, u, j:j + 1], axis=0),
                                            in_=stage[0:EP, u, j, :], in_offset=None).then_inc(scattered[u], 16)

            pool.wait_ge(pads_stored, 16 * (NT // PS_PAD))
            for u in range(2):
                scatter(0, u)
            with pool.Fori(1, SI) as i:
                for u in range(2):
                    scatter(i, u)

            def scatter2(i, u):
                hold(pool, "pool", (pair_staged[u], (i + 1) * 32))
                for j in range(SU2):
                    scatter_pair(u, j)

            def scatter_pair(u, j):
                pool.indirect_dma_start(out=rec2_rows, out_offset=bass.IndirectOffsetOnAxis(ap=stage2_i[0:EP, u, j:j + 1], axis=0),
                                        in_=stage2[0:EP, u, j:j + 1], in_offset=None).then_inc(pair_scattered[u], 16)

            def scatter_later(i, k):
                u, j = k // R8, k % R8
                if j == 0:
                    hold(pool, "pool", (pair_staged[u], (i + SI2_EARLY + 1) * 32))
                for n in range(2 * SU2 // RING):
                    scatter_pair(u, j * (2 * SU2 // RING) + n)

            pool.wait_ge(pairs_stored, 16)
            for u in range(2):
                scatter2(0, u)
            with pool.Fori(1, SI2_EARLY) as i:
                for u in range(2):
                    scatter2(i, u)

            def gather(tab, w, pass_no, also=None):
                hold(pool, "pool", (table_stored, (pass_no + 1) * 16))
                base = pass_no * (NG + 1)

                def step(g, s):
                    n = base + 1 if isinstance(g, int) and g < RING else base + g - RING + 2
                    hold(pool, "pool", (idx_staged, n))
                    for t in range(GT):
                        pool.indirect_dma_start(out=rows4[:, s, t, 0:w], out_offset=None, in_=tab,
                                                in_offset=bass.IndirectOffsetOnAxis(ap=ids[:, s * GT + t:s * GT + t + 1], axis=0)).then_inc(gathered[s], 16)
                walk(pool, [(0, step)], also=also)

            gather(tab_g, TG, 0, scatter_later)
            with pool.Fori(0, L) as l:
                gather(tab_a, TA, l + 1)
            pool.wait_ge(emb_used, 1)
            gather_emb(a["L2_gnn_emb"])
            gather(tab_c, TC, L + 1)
            gather(tab_c, TC, L + 2)
            gather(tab_g, TG, L + 3)
            gather(tab_c, TC, L + 4)

        def got(pass_no, g, s):
            return (pass_no * (NG // RING) + 1) * (16 * GT) + (g - s) * (16 * GT // RING)

        def got_ea(pass_no, g, s):
            return (pass_no * (NG // R8) + 1) * 16 + (g - s % R8) * (16 // R8)

        @block.scalar
        def _(act):
            def put(i, u):
                if not (isinstance(i, int) and i == 0):
                    hold(act, "act", (scattered[u], i * (16 * SU)))
                cols = bass.ds(i * (2 * SU) + u * SU, SU)
                act.activation(stage_i[0:EP, u, :], row_s[:, cols], ACT.Copy).then_inc(rec_parts, 1)
                act.activation(stage[0:EP, u, :, C_W], w_e[:, cols], ACT.Copy).then_inc(rec_parts, 1)
                act.activation(stage[0:EP, u, :, C_KEY], krel_e[:, cols], ACT.Copy).then_inc(rec_parts, 1)
                act.activation(stage[0:EP, u, :, C_IDX], oth_e[:, cols], ACT.Copy).then_inc(rec_parts, 1)
                act.wait_ge(rec_parts, i * 8 + 4 * u + 4)
                act.sem_inc(rec_staged, 1)

            act.wait_ge(params_loaded, PARAMS * 16)
            act.wait_ge(cols_ready, 2)
            act.wait_ge(wmu_made, 1)
            act.activation(wmu, ps_s[0:H, 0, 0:L * H], ACT.Copy).then_inc(wmu_copied, 1)
            act.wait_ge(rows_placed, 1)
            for u in range(2):
                put(0, u)
            with act.Fori(1, SI) as i:
                for u in range(2):
                    put(i, u)

            class At:
                ln = proj = turn = 0

            def std(n):
                act.wait_ge(ln_var, At.ln + 1)
                act.activation(ln_c[:, 0:n], ln_b[:, 0:n], ACT.Sqrt, bias=eps[:, 0:1], scale=1.0 / H).then_inc(ln_std, 1)
                At.ln = At.ln + 1

            def project(k):
                b0 = At.proj * NB7
                with act.Fori(0, NB7) as j:
                    act.wait_ge(proj_t, b0 + j + 1)
                    act.activation(xt_sb[0:k, :], ps[0:k, 0:NB7 * P], ACT.Copy).then_inc(proj_evac, 1)
                At.proj = At.proj + 1

            def turned(k):
                b0 = At.turn * NB7
                with act.Fori(0, NB7) as j:
                    hold(act, "act", (turn_t, b0 + j + 1))
                    act.activation(qt[0:k, bass.ds(j * (NB7 * P), NB7 * P)], ps[0:k, 0:NB7 * P], ACT.Copy).then_inc(turn_evac, 1)
                hold(act, "act", (turn_evac, b0 + NB7))
                At.turn = At.turn + 1

            act.wait_ge(angle_ready, 1)
            act.activation(cut_w[:, :], cut_w[:, :], ACT.Sin, bias=half_pi[:, 0:1], scale=-PI / CUT).then_inc(cosine_done, 1)
            act.activation(logm[:, :], logm[:, :], ACT.Ln).then_inc(cosine_done, 1)

            def gated(c):
                base = c * NG

                def evac(g, s):
                    r, par = s % 4, s % 2
                    act.wait_ge(gate["t"], base + g + 1)
                    if c == 0:
                        act.activation(eat[0:R, r * GS:(r + 1) * GS], ps_t[0:R, par, 0:GS], ACT.Copy).then_inc(gate["evac"], 1)
                    act.activation(ebt[0:G, r * GS:(r + 1) * GS], ps_t[0:G, par, GS:2 * GS], ACT.Copy).then_inc(gate["evac_e"], 1)
                    again(act, gate["agg"], base, g, R8)
                    act.activation(msg4[:, s % R8, :, H], rows4[:, s, :, H], ACT.Copy).then_inc(gate["mj"], 1)

                def silu(g, s):
                    r, par = s % 4, s % 2
                    act.wait_ge(gate["hid"], base + g + 1)
                    again(act, gate["out"], base, g, 4)
                    act.activation(hid[0:W96, r * GS:(r + 1) * GS], ps_s[0:W96, par, 0:GS], ACT.Silu,
                                   bias=fb1[:, 0:1]).then_inc(gate["act"], 1)

                walk(act, [(2, silu), (0, evac)] if c == 0 else [(0, evac)])

            def attention(base):
                def evac(g, s, b):
                    r, par = s % 4, s % 2
                    act.activation(qcur[0:H + 1, r * P:(r + 1) * P], qt[0:H + 1, bass.ds(b * P, P)], ACT.Copy).then_inc(att["q"], 1)
                    act.wait_ge(att["kt"], base + g + 1)
                    if not (isinstance(g, int) and g < BACK - TURN):
                        act.wait_ge(att["pt"], base + g + 1 - (BACK - TURN))
                    act.activation(kturn[0:H + 1, r * GS:(r + 1) * GS], ps_t[0:H + 1, par, 0:GS], ACT.Copy).then_inc(att["kt_evac"], 1)

                def exps(g, s, _):
                    r = s % 4
                    act.wait_ge(att["rdif"], base + g + 1)
                    act.activation(decay[:, s % R8:s % R8 + 1], rdif[:, s % R8:s % R8 + 1], ACT.Exp).then_inc(att["decay"], 1)
                    act.activation(prob[:, r * GS:(r + 1) * GS], ps_q[:, r, 0:GS], ACT.Exp,
                                   bias=nmn[:, s % R8:s % R8 + 1]).then_inc(att["probs"], 1)

                def back(g, s, _):
                    r, par = s % 4, s % 2
                    act.wait_ge(att["pt"], base + g + 1)
                    again(act, att["agg"], base, g, 4)
                    act.activation(probt[:, r * GS:(r + 1) * GS], ps_t[:, par, GS:2 * GS], ACT.Copy).then_inc(att["pt_evac"], 1)

                walk(act, [(4, exps), (TURN, evac), (BACK, back)], (nc, ACT_ENGINE, blk_s))

            project(G)
            turned(G)
            std(NB)
            gated(0)
            std(NB)
            p0, t0, n0 = At.proj, At.turn, At.ln
            with act.Fori(0, L) as l:
                At.proj, At.turn, At.ln = l * LAYER_PROJ + p0, l * LAYER_TURN + t0, l * LAYER_LN + n0
                project(H)
                std(2 * NB)
                turned(H)
                attention(l * NG)
                project(W96)
                std(NB)
            At.proj, At.turn, At.ln = L * LAYER_PROJ + p0, L * LAYER_TURN + t0, L * LAYER_LN + n0
            std(NB)
            project(W96)
            project(W96)
            project(G)
            turned(G)
            std(NB)
            gated(1)
            std(NB)
            std(NB)
            act.wait_ge(degree_ready, 1)
            act.activation(deg[:, :], deg[:, :], ACT.Sqrt).then_inc(degree_root, 1)
            project(H)

        @block.tensor
        def _(pe):
            pe.wait_ge(consts_ready, 7)
            pe.wait_ge(params_loaded, PARAMS * 16)
            for l in range(L):
                last = pe.matmul(ps_s[0:H, 0, l * H:(l + 1) * H], wm_t[:, l * H:(l + 1) * H], wub[:, l * H:(l + 1) * H],
                                 start=True, stop=True)
            last.then_inc(wmu_made, 1)
            for n in range(2):
                pe.wait_ge(counts_ready, n + 1)
                pe.matmul(ps_p[:, 0, 0:NB], ones[0:EP, :], cnt[0:EP, :], start=True, stop=True)
                pe.matmul(ps_p[0:EP, 1, 0:NB], tri[0:EP, 0:EP], cnt[0:EP, :], start=True, stop=True).then_inc(sums_ready, 1)

            class At:
                x = proj = turn = 0

            def turn_blocks(src, j):
                for i in range(NB7):
                    last = pe.transpose(ps[0:W96, i * P:(i + 1) * P], src[:, (j * NB7 + i) * W96:(j * NB7 + i + 1) * W96], ident[:, :])
                return last

            def project(src, k, w, n):
                hold(pe, "pe", (x_ready, At.x + 1))
                b0 = At.proj * NB7
                for j in range(NB7):
                    turn_blocks(src, j).then_inc(proj_t, 1)
                    pe.wait_ge(proj_evac, b0 + j + 1)
                    for i in range(NB7):
                        last = pe.matmul(ps[:, 4 * 512 + i * P:4 * 512 + i * P + n], xt_sb[0:k, i * P:(i + 1) * P], w,
                                         start=True, stop=True)
                    last.then_inc(proj_mm, 1)
                    hold(pe, "pe", (proj_out, b0 + j + 1))
                At.proj, At.x = At.proj + 1, At.x + 1

            def turned(src):
                hold(pe, "pe", (x_ready, At.x + 1))
                b0 = At.turn * NB7
                for j in range(NB7):
                    turn_blocks(src, j).then_inc(turn_t, 1)
                    hold(pe, "pe", (turn_evac, b0 + j + 1))
                At.turn, At.x = At.turn + 1, At.x + 1

            def gated(c, pass_no):
                base = c * NG

                def turn(g, s, _):
                    par = s % 2
                    pe.wait_ge(gathered[s], got(pass_no, g, s))
                    if c == 0:
                        pe.wait_ge(ea_loaded[s % R8], got_ea(0, g, s))
                    again(pe, gate["evac_e"], base, g, 2)
                    pe.sem_inc(tick["pe"], 1)
                    for t in range(GT if c == 0 else 0):
                        pe.transpose(ps_t[0:R, par, t * P:(t + 1) * P], ear4[:, s % R8, t, 0:R], ident[:, :])
                    for t in range(GT):
                        last = pe.transpose(ps_t[0:G, par, GS + t * P:GS + (t + 1) * P], rows4[:, s, t, H + 1:TG], ident[:, :])
                    last.then_inc(gate["t"], 1)

                def first(g, s, b):
                    r, par = s % 4, s % 2
                    if c == 0:
                        pe.wait_ge(gate["evac"], base + g + 1)
                        again(pe, gate["act"], base, g, 2)
                        pe.sem_inc(tick["pe"], 1)
                        pe.matmul(ps_s[0:W96, par, 0:GS], f1[:, :], eat[0:R, r * GS:(r + 1) * GS],
                                  start=True, stop=True).then_inc(gate["hid"], 1)
                    hold(pe, "pe", (gate["evac_e"], base + g + 1))
                    if not (isinstance(g, int) and g < 2):
                        hold(pe, "pe", (gate["logit"], base + g - 1))
                    for t in range(GT):
                        last = pe.matmul(ps_p[:, par, t * P:(t + 1) * P], ebt[0:G, r * GS + t * P:r * GS + (t + 1) * P],
                                         qt[0:G, bass.ds(b * P, P)], start=True, stop=True)
                    last.then_inc(gate["bil"], 1)

                def second(g, s, _):
                    r, par = s % 4, s % 2
                    pe.wait_ge(gate["act"], base + g + 1)
                    again(pe, gate["msg"], base, g, 2)
                    again(pe, gate["kept"], base, g, 2)
                    for t in range(GT):
                        last = pe.matmul(ps_a[:, par, P + t * W96:P + (t + 1) * W96], hid[0:W96 + 1, r * GS + t * P:r * GS + (t + 1) * P],
                                         f2[:, :], start=True, stop=True)
                    last.then_inc(gate["out"], 1)

                def total(g, s, _):
                    par = s % 2
                    pe.wait_ge(gate["msg"], base + g + 1)
                    pe.wait_ge(gate["mj"], base + g + 1)
                    again(pe, gate["acc"], base, g, 2)
                    for t in range(GT):
                        last = pe.matmul(ps_a[:, par, 0:TC], hot4[:, s % R8, t, :], msg4[:, s % R8, t, :], start=t == 0, stop=t == GT - 1)
                    last.then_inc(gate["agg"], 1)

                walk(pe, [(5, total), (3, second), (0, turn), (1, first)] if c == 0 else [(5, total), (0, turn), (1, first)],
                     (nc, PE_ENGINE, blk_s))

            def attention(base, pass_no):
                def turn(g, s):
                    par = s % 2
                    pe.wait_ge(att["keys"], base + g + 1)
                    again(pe, att["kt_evac"], base, g, 2)
                    again(pe, att["pt_evac"], base, g, 2 + BACK - TURN)
                    pe.sem_inc(tick["pe"], 1)
                    for t in range(GT):
                        last = pe.transpose(ps_t[0:H + 1, par, t * P:(t + 1) * P], rows4[:, s, t, 0:H + 1], ident[:, :])
                    last.then_inc(att["kt"], 1)

                def scores(g, s):
                    r = s % 4
                    pe.wait_ge(att["q"], base + g + 1)
                    pe.wait_ge(att["kt_evac"], base + g + 1)
                    pe.wait_ge(att["mask"], base + g + 1)
                    again(pe, att["probs"], base, g, 4)
                    for t in range(GT):
                        pe.matmul(ps_q[:, r, t * P:(t + 1) * P], qcur[0:H + 1, r * P:(r + 1) * P],
                                  kturn[0:H + 1, r * GS + t * P:r * GS + (t + 1) * P], start=True, stop=False)
                        last = pe.matmul(ps_q[:, r, t * P:(t + 1) * P], nothot4[:, r, t, :], neg_i[:, :],
                                         start=False, stop=True)
                    last.then_inc(att["scores"], 1)

                def back(g, s):
                    r, par = s % 4, s % 2
                    pe.wait_ge(att["probs"], base + g + 1)
                    again(pe, att["pt_evac"], base, g, 2)
                    for t in range(GT):
                        last = pe.transpose(ps_t[:, par, GS + t * P:GS + (t + 1) * P], prob[:, r * GS + t * P:r * GS + (t + 1) * P], ident[:, :])
                    last.then_inc(att["pt"], 1)

                def total(g, s):
                    r, par = s % 4, s % 2
                    pe.wait_ge(att["pt_evac"], base + g + 1)
                    again(pe, att["acc"], base, g, 2)
                    for t in range(GT):
                        last = pe.matmul(ps_a[:, par, 0:TC], probt[:, r * GS + t * P:r * GS + (t + 1) * P],
                                         rows4[:, s, t, H + 1:TA], start=t == 0, stop=t == GT - 1)
                    last.then_inc(att["agg"], 1)

                walk(pe, [(TURN, turn), (BACK, back), (2, scores), (6, total)])

            def summed(c, pass_no):
                base = c * NG

                def total(g, s):
                    par = s % 2
                    pe.wait_ge(gathered[s], got(pass_no, g, s))
                    pe.wait_ge(conv["hot"], base + g + 1)
                    again(pe, conv["acc"], base, g, 2)
                    for t in range(GT):
                        last = pe.matmul(ps_a[:, par, 0:TC], hot4[:, s % R8, t, :], rows4[:, s, t, 0:TC], start=t == 0, stop=t == GT - 1)
                    last.then_inc(conv["agg"], 1)

                walk(pe, [(1, total)])

            project(z, G, adp[0][:, :], G)
            turned(yq)
            gated(0, 0)
            p0, t0, x0 = At.proj, At.turn, At.x
            with pe.Fori(0, L) as l:
                At.proj, At.turn, At.x = l * LAYER_PROJ + p0, l * LAYER_TURN + t0, l * LAYER_X + x0
                project(z, H, wqk_c[:, :], W96)
                turned(yq)
                attention(l * NG, l + 1)
                project(z, W96, ww_c[:, :], H)
            At.proj, At.turn, At.x = L * LAYER_PROJ + p0, L * LAYER_TURN + t0, L * LAYER_X + x0
            summed(0, L + 1)
            project(z, W96, wc[0][:, :], H)
            summed(1, L + 2)
            project(z, W96, wc[1][:, :], H)
            project(z, G, adp[1][:, :], G)
            turned(yq)
            gated(1, L + 3)
            summed(2, L + 4)
            project(z, H, w3[:, :], H)

        @block.vector
        def _(dve):
            do = Chain(dve, node_done)
            do(dve.memset(ring[:, 3200:3200 + 2 * SU * RW], 0.0))
            dve.memset(f2[:, :], 0.0).then_inc(f2_cleared, 1)
            dve.memset(eps[:, :], 1e-5).then_inc(cols_ready, 1)
            dve.memset(half_pi[:, :], PI / 2).then_inc(cols_ready, 1)
            padv = pads[:, 0:PS_PAD * RW].rearrange("p (t c) -> p t c", c=RW)
            do(dve.memset(pads, 0.0))
            dve.memset(padv[:, :, C_KEY], PAD).then_inc(pads_ready, 1)
            dve.wait_ge(iota_ready, 1)
            do(dve.tensor_copy(ioc[:, :], ioi[:, 0:P]))
            do(dve.tensor_copy(iog, ioi[0:1, :]))

            def slots(key_i, rel, row, blk, n):
                do(dve.tensor_scalar(t1.bitcast(I32), key_i, 7, None, ALU.logical_shift_right))
                do(dve.tensor_copy(bf, t1.bitcast(I32)))
                do(dve.tensor_scalar(t1.bitcast(I32), key_i, P - 1, None, ALU.bitwise_and))
                do(dve.tensor_copy(rel, t1.bitcast(I32)))
                for c in range(NB):
                    do(dve.tensor_scalar(t1, bf, float(c), None, ALU.is_equal, ALU.add, accum_out=cnt[0:EP, c:c + 1]))
                dve.sem_inc(counts_ready, 1)
                dve.wait_ge(sums_ready, n + 1)
                do(dve.tensor_scalar(gi[:, :], ps_p[:, 0, 0:NB], float(GS - 1), None, ALU.add))
                do(dve.tensor_scalar(gi[:, :], gi[:, :], 8, None, ALU.logical_shift_right))
                do(dve.tensor_copy(gf[:, :], gi[:, :]))
                do(dve.tensor_tensor_scan(incl[:, :], gf[:, :], zero49[:, :], 0.0, ALU.add, ALU.add))
                do(dve.tensor_tensor(base[:, :], incl[:, :], gf[:, :], ALU.subtract))
                do(dve.tensor_scalar(base[:, :], base[:, :], float(GS), -1.0, ALU.mult, ALU.add))
                do(dve.tensor_tensor(base[0:EP, :], base[0:EP, :], ps_p[0:EP, 1, 0:NB], ALU.add))
                do(dve.memset(pos, 0.0))
                do(dve.memset(blf, 0.0))
                do.base = do.base + do.n
                do.n = 0
                b0 = do.base
                with dve.Fori(0, NB) as c:
                    do.base, do.n = c * 5 + b0, 0
                    col = bass.ds(c, 1)
                    do(dve.tensor_scalar(t1, bf, iocf[0:EP, col], None, ALU.is_equal))
                    do(dve.tensor_tensor_scan(t2, t1, zero_e, base[0:EP, col], ALU.add, ALU.add))
                    do(dve.tensor_tensor(t1, t1, t2, ALU.mult))
                    do(dve.tensor_tensor(pos, pos, t1, ALU.add))
                    do(dve.scalar_tensor_tensor(blf, iog, incl[0:1, col], blf, ALU.is_ge, ALU.add))
                do.base, do.n = b0 + NB * 5, 0
                do(dve.tensor_scalar(blk[:, :], blf, float(NB - 1), None, ALU.min))
                do(dve.tensor_copy(t1.bitcast(I32), pos))
                do(dve.tensor_scalar(t2.bitcast(I32), t1.bitcast(I32), P - 1, None, ALU.bitwise_and))
                do(dve.tensor_scalar(pos.bitcast(I32), t1.bitcast(I32), 7, None, ALU.logical_shift_right))
                do(dve.scalar_tensor_tensor(row, t2.bitcast(I32), float(NT), pos.bitcast(I32), ALU.mult, ALU.add))

            iocf = ioc
            zero49 = z1
            do(dve.memset(zero49[:, :], 0.0))
            do(dve.memset(zero_e, 0.0))
            dve.wait_ge(ints_loaded, 48)
            do(dve.tensor_copy(oth_e, dst_i))
            slots(src_i, krel_e, row_s, blk_s, 0)
            dve.sem_inc(rows_placed, 1)
            dve.wait_ge(pads_stored, 16 * (NT // PS_PAD))
            do(dve.memset(pads[:, 0:NT], PAD))
            dve.sem_inc(pairs_ready, 1)
            slots(dst_i, pair_e, row_d, blk_d, 1)
            do(dve.tensor_copy(t1, src_i))
            do(dve.scalar_tensor_tensor(pair_e, t1, float(PACK), pair_e, ALU.mult, ALU.add))
            dve.sem_inc(pairs_placed, 1)
            for c in range(NT // XT):
                dve.wait_ge(chunk_loaded[c % 2], 16 * (c // 2 + 1))
                v = (z, yq)[c % 2][:, 0:XT * RW].rearrange("p (t c) -> p t c", c=RW)
                o = slice(c * XT, (c + 1) * XT)
                do(dve.tensor_copy(idx_s[:, o], v[:, :, C_IDX]))
                do(dve.tensor_copy(key_s[:, o], v[:, :, C_KEY]))
                do(dve.tensor_copy(cut_w[:, o], v[:, :, C_W]))
                dve.sem_inc(chunk_used, 1)
            do(dve.memset(idx_s[:, NT:NT + 2 * RING], 0))
            keep = acc[:, 0:NT]
            do(dve.tensor_scalar(keep, cut_w[:, :], CUT, 0.5, ALU.is_lt, ALU.mult))
            do(dve.tensor_scalar(yq[:, 0:NT], cut_w[:, :], -1.0, None, ALU.mult))
            do(dve.tensor_tensor(cut_w[:, :], cut_w[:, :], yq[:, 0:NT], ALU.max))
            do(dve.tensor_scalar(cut_w[:, :], cut_w[:, :], CUT, None, ALU.min))
            do(dve.memset(xs3[:, NB - 1, :], 0.0))
            dve.sem_inc(x_cleared, 1)
            dve.wait_ge(nodes_loaded, 64)
            do(dve.tensor_scalar(logm[:, :], mult[:, :], 1.0, None, ALU.max))
            dve.sem_inc(angle_ready, 1)
            do(dve.memset(z[:, :], 0.0))
            do(dve.memset(yq[:, :], 0.0))
            dve.wait_ge(cosine_done, 2)
            do(dve.scalar_tensor_tensor(cut_w[:, :], cut_w[:, :], 1.0, keep, ALU.add, ALU.mult))
            do(dve.memset(qt[:, :], 1.0))
            do(dve.memset(hid[0:W96 + 1, :], 1.0))

            class At:
                ln = proj = turn = 0

            def bc(v, w=NB):
                return v.unsqueeze(2).to_broadcast([P, w, H])

            def wide(v, w=H):
                return v.unsqueeze(1).to_broadcast([P, NB, w])

            def norm(src, dst, w=NB, relu=False):
                xc = tabs[:, 0:w * H].rearrange("p (b c) -> p b c", c=H)
                do(dve.tensor_reduce(ln_a[:, 0:w], src, AX.X, ALU.add))
                do(dve.tensor_scalar(ln_a[:, 0:w], ln_a[:, 0:w], 1.0 / H, None, ALU.mult))
                do(dve.tensor_tensor(xc, src, bc(ln_a[:, 0:w], w), ALU.subtract))
                do(dve.tensor_tensor(dst, xc, xc, ALU.mult))
                do(dve.tensor_reduce(ln_b[:, 0:w], dst, AX.X, ALU.add))
                dve.sem_inc(ln_var, 1)
                dve.wait_ge(ln_std, At.ln + 1)
                do(dve.reciprocal(ln_d[:, 0:w], ln_c[:, 0:w]))
                if relu:
                    do(dve.scalar_tensor_tensor(dst, xc, 0.0, bc(ln_d[:, 0:w], w), ALU.max, ALU.mult))
                else:
                    do(dve.tensor_tensor(dst, xc, bc(ln_d[:, 0:w], w), ALU.mult))
                At.ln = At.ln + 1

            def projected(n):
                b0 = At.proj * NB7
                with dve.Fori(0, NB7) as j:
                    hold(dve, "dve", (proj_mm, b0 + j + 1))
                    dve.tensor_copy(yq3[:, bass.ds(j * NB7, NB7), 0:n],
                                    ps[:, 4 * 512:4 * 512 + NB7 * P].rearrange("p (b c) -> p b c", c=P)[:, :, 0:n]).then_inc(proj_out, 1)
                At.proj = At.proj + 1
                dve.wait_ge(proj_out, b0 + NB7)

            def begin(idx):
                do(dve.memset(acc[:, :], 0.0))
                dve.tensor_copy(ids[:, :], idx[:, 0:RING * GT]).then_inc(idx_staged, 1)

            def add_up(sums, base, idx, scale):
                def step(g, s, b):
                    o = acc[:, bass.ds(b * TC, TC)]
                    dve.wait_ge(sums["agg"], base + g + 1)
                    again(dve, sums["acc"], base, g, 1)
                    if scale is None:
                        dve.tensor_tensor(o, o, ps_a[:, s % 2, 0:TC], ALU.add).then_inc(sums["acc"], 1)
                    else:
                        dve.wait_ge(sums["decay"], base + g + 1)
                        dve.scalar_tensor_tensor(o, o, scale[:, s % R8:s % R8 + 1], ps_a[:, s % 2, 0:TC], ALU.mult, ALU.add).then_inc(sums["acc"], 1)
                    dve.tensor_copy(ids[:, s * GT:(s + 1) * GT], idx[:, bass.ds(g * GT + RING * GT, GT)]).then_inc(idx_staged, 1)
                return step

            def one_hot(key, g, s, dst, op):
                return dve.tensor_tensor(dst, ioc[:, :].unsqueeze(1).to_broadcast([P, GT, P]),
                                         key[:, bass.ds(g * GT, GT)].unsqueeze(2).to_broadcast([P, GT, P]), op)

            def gated(c, pass_no):
                base = c * NG

                def front(g, s, _):
                    one_hot(key_s, g, s, hot4[:, s % R8], ALU.is_equal).then_inc(gate["hot"], 1)
                    dve.wait_ge(gathered[s], got(pass_no, g, s))
                    dve.tensor_tensor(hcut4[:, s % R8], rows4[:, s, :, 0:H],
                                      cut_w[:, bass.ds(g * GT, GT)].unsqueeze(2).to_broadcast([P, GT, H]), ALU.mult).then_inc(gate["hcut"], 1)

                def logits(g, s, _):
                    dve.wait_ge(gate["bil"], base + g + 1)
                    dve.wait_ge(gate["hot"], base + g + 1)
                    for t in range(GT):
                        last = dve.tensor_tensor_reduce(out=junk[:, (s % 4) * GS + t * P:(s % 4) * GS + (t + 1) * P], in0=hot4[:, s % R8, t, :], in1=ps_p[:, s % 2, t * P:(t + 1) * P],
                                                        scale=1.0, scalar=0.0, op0=ALU.mult, op1=ALU.add,
                                                        accum_out=logit[:, s % R8 * GT + t:s % R8 * GT + t + 1])
                    last.then_inc(gate["logit"], 1)

                def message(g, s, _):
                    if c == 0:
                        dve.wait_ge(gate["out"], base + g + 1)
                        if not (isinstance(g, int) and g < 4):
                            dve.wait_ge(gates_stored[s % 4], (g - s % 4) * (16 // 4))
                        both = ps_a[:, s % 2, P:P + GT * W96].rearrange("p (t c) -> p t c", c=W96)
                        dve.tensor_copy(kept4[:, s % 4, :].rearrange("p (t c) -> p t c", c=H), both[:, :, H:W96]).then_inc(gate["kept"], 1)
                        gates = [both[:, t, 0:H] for t in range(GT)]
                    else:
                        dve.wait_ge(ea_loaded[s % R8], got_ea(L + 1, g, s))
                        gates = [gear4[:, s % R8, t, :] for t in range(GT)]
                    dve.wait_ge(gate["hcut"], base + g + 1)
                    dve.wait_ge(gate["logit"], base + g + 1)
                    for t in range(GT):
                        last = dve.scalar_tensor_tensor(msg4[:, s % R8, t, 0:H], gates[t],
                                                        logit[:, s % R8 * GT + t:s % R8 * GT + t + 1], hcut4[:, s % R8, t, :], ALU.add, ALU.mult)
                    last.then_inc(gate["msg"], 1)

                walk(dve, [(0, front), (2, logits), (4, message), (6, add_up(gate, base, idx_s, None))], (nc, DVE_ENGINE, blk_s))
                dve.wait_ge(gate["acc"], base + NG)

            def attention(base, pass_no):
                def front(g, s, _):
                    r = s % 4
                    one_hot(key_s, g, s, nothot4[:, r], ALU.not_equal).then_inc(att["mask"], 1)
                    dve.wait_ge(gathered[s], got(pass_no, g, s))
                    dve.wait_ge(ea_loaded[s % R8], got_ea(pass_no, g, s))
                    dve.scalar_tensor_tensor(rows4[:, s, :, 0:R], ear4[:, s % R8, :, 0:R], 0.1, rows4[:, s, :, 0:R],
                                             ALU.mult, ALU.add).then_inc(att["keys"], 1)

                def peak(g, s, b):
                    dve.wait_ge(att["scores"], base + g + 1)
                    dve.tensor_reduce(gmax[:, s % R8:s % R8 + 1], ps_q[:, s % 4, 0:GS], AX.X, ALU.max, negate=True).then_inc(att["gmax"], 1)
                    dve.wait_ge(att["gmax"], base + g + 1)
                    again(dve, att["saved"], base, g, 1)
                    dve.tensor_tensor(nmn[:, s % R8:s % R8 + 1], gmax[:, s % R8:s % R8 + 1], nmax[:, bass.ds(b, 1)], ALU.min).then_inc(att["nmn"], 1)
                    dve.wait_ge(att["nmn"], base + g + 1)
                    dve.tensor_tensor(rdif[:, s % R8:s % R8 + 1], nmn[:, s % R8:s % R8 + 1], nmax[:, bass.ds(b, 1)], ALU.subtract).then_inc(att["rdif"], 1)
                    dve.wait_ge(att["rdif"], base + g + 1)
                    dve.tensor_tensor(nmax[:, bass.ds(b, 1)], gmax[:, s % R8:s % R8 + 1], nmax[:, bass.ds(b, 1)], ALU.min).then_inc(att["saved"], 1)

                walk(dve, [(0, front), (3, peak), (7, add_up(att, base, idx_s, decay))], (nc, DVE_ENGINE, blk_s))
                dve.wait_ge(att["acc"], base + NG)

            def summed(c):
                base = c * NG

                def front(g, s, _):
                    one_hot(key_d, g, s, hot4[:, s % R8], ALU.is_equal).then_inc(conv["hot"], 1)

                walk(dve, [(0, front), (3, add_up(conv, base, idx_d, None))], (nc, DVE_ENGINE, blk_d))
                dve.wait_ge(conv["acc"], base + NG)

            def gated_table():
                tg = blocks(tabs, TG)
                do(dve.tensor_copy(z3[:, :, 0:G], emb3))
                dve.sem_inc(x_ready, 1)
                projected(G)
                dve.sem_inc(x_ready, 1)
                dve.wait_ge(turn_evac, At.turn)
                norm(xs3, z3[:, :, 0:H], relu=True)
                do(dve.tensor_tensor(tg[:, :, 0:H], z3[:, :, 0:H], bc(mult[:, :]), ALU.mult))
                do(dve.tensor_copy(tg[:, :, H], mult[:, :]))
                do(dve.tensor_copy(tg[:, :, H + 1:TG], emb3))
                dve.sem_inc(table_ready, 1)
                begin(idx_s)

            def gated_end(gain, shift):
                do(dve.tensor_scalar(ln_a[:, 0:NB], acc3[:, :, H], 1e-8, None, ALU.max))
                do(dve.reciprocal(ln_a[:, 0:NB], ln_a[:, 0:NB]))
                do(dve.tensor_tensor(yq3[:, :, 0:H], acc3[:, :, 0:H], bc(ln_a[:, 0:NB]), ALU.mult))
                do(dve.tensor_tensor(yq3[:, :, 0:H], yq3[:, :, 0:H], z3[:, :, 0:H], ALU.add))
                norm(yq3[:, :, 0:H], z3[:, :, 0:H])
                do(dve.tensor_tensor(z3[:, :, 0:H], z3[:, :, 0:H], wide(gain), ALU.mult))
                do(dve.tensor_tensor(z3[:, :, 0:H], z3[:, :, 0:H], wide(shift), ALU.add))

            def conv_table():
                tc = blocks(tabs, TC)
                do(dve.tensor_copy(tc[:, :, 0:H], z3[:, :, 0:H]))
                do(dve.memset(tc[:, :, H], 1.0))
                dve.sem_inc(table_ready, 1)
                begin(idx_d)

            dve.wait_ge(params_loaded, PARAMS * 16)
            dve.wait_ge(wmu_moved, 16)
            dve.wait_ge(nodes_loaded, 96)
            dve.wait_ge(emb_gathered, 16 * NB)
            At.turn = NB7
            gated_table()
            gated(0, 0)
            dve.sem_inc(emb_used, 1)
            gated_end(vec["gn"][:, :], vec["bn"][:, :])
            ta = blocks(tabs, TA)
            b0 = do.base + do.n
            p0, n0 = At.proj, At.ln
            with dve.Fori(0, L) as l:
                do.base, do.n = l * LAYER_CHAIN + b0, 0
                At.proj, At.ln = l * LAYER_PROJ + p0, l * LAYER_LN + n0
                for cur, every, w in ((lcur, lpar, 6 * H), (wqk_c, wqk, W96), (ww_c, ww, H)):
                    dve.tensor_copy(cur[:, :], every[:, bass.ds(l * w, w)]).then_inc(node_done, 1)
                do.n = 3
                dve.wait_ge(node_done, do.base + 3)
                dve.sem_inc(x_ready, 1)
                projected(W96)
                qk = yq[:, :].rearrange("p (b c) -> p b c", c=H)
                norm(qk, qk, 2 * NB)
                do(dve.tensor_tensor(yq3, yq3, wide(lcur[:, 0:W96], W96), ALU.mult))
                do(dve.tensor_tensor(yq3[:, :, 0:H], yq3[:, :, 0:H], wide(lcur[:, W96:3 * H]), ALU.add))
                dve.sem_inc(x_ready, 1)
                do(dve.tensor_tensor(ta[:, :, 0:H], yq3[:, :, H:W96], wide(lcur[:, 3 * H:4 * H]), ALU.add))
                do(dve.tensor_copy(ta[:, :, H], logm[:, :]))
                do(dve.tensor_copy(ta[:, :, H + 1:TA - 1], z3[:, :, 0:H]))
                do(dve.memset(ta[:, :, TA - 1], 1.0))
                dve.sem_inc(table_ready, 1)
                do(dve.memset(nmax[:, :], 1e20))
                begin(idx_s)
                attention(l * NG, l + 1)
                do(dve.tensor_scalar(ln_a[:, 0:NB], acc3[:, :, H], 1e-10, None, ALU.add))
                do(dve.reciprocal(ln_a[:, 0:NB], ln_a[:, 0:NB]))
                do(dve.tensor_tensor(z3[:, :, H:W96], acc3[:, :, 0:H], bc(ln_a[:, 0:NB]), ALU.mult))
                dve.sem_inc(x_ready, 1)
                projected(H)
                do(dve.scalar_tensor_tensor(yq3[:, :, 0:H], yq3[:, :, 0:H], 0.01, yq3[:, :, 0:H], ALU.mult, ALU.max))
                do(dve.tensor_tensor(yq3[:, :, 0:H], yq3[:, :, 0:H], z3[:, :, 0:H], ALU.add))
                norm(yq3[:, :, 0:H], z3[:, :, 0:H])
                do(dve.tensor_tensor(z3[:, :, 0:H], z3[:, :, 0:H], wide(lcur[:, 4 * H:5 * H]), ALU.mult))
                do(dve.tensor_tensor(z3[:, :, 0:H], z3[:, :, 0:H], wide(lcur[:, 5 * H:6 * H]), ALU.add))
                dve.sem_inc(tick["dve"], 1)
                assert do.n == LAYER_CHAIN, do.n
            do.base, do.n = b0 + L * LAYER_CHAIN, 0
            At.proj, At.ln = L * LAYER_PROJ + p0, L * LAYER_LN + n0
            do(dve.tensor_tensor(xs3, xs3, z3[:, :, 0:H], ALU.add))
            norm(xs3, z3[:, :, 0:H], relu=True)
            dve.sem_inc(tabs_free, 1)
            dve.wait_ge(pairs_loaded, 16)
            pair_i = tabs[:, NT:2 * NT].bitcast(I32)
            do(dve.tensor_copy(pair_i, pair_l))
            do(dve.tensor_scalar(pair_l.bitcast(I32), pair_i, PACK - 1, None, ALU.bitwise_and))
            do(dve.tensor_copy(key_d[:, :], pair_l.bitcast(I32)))
            do(dve.tensor_scalar(idx_d[:, 0:NT], pair_i, 8, None, ALU.logical_shift_right))
            do(dve.memset(idx_d[:, NT:NT + 2 * RING], 0))
            conv_table()
            summed(0)
            do(dve.tensor_scalar(deg[:, :], acc3[:, :, H], 1.0, None, ALU.add))
            do(dve.tensor_copy(z3[:, :, H:W96], acc3[:, :, 0:H]))
            dve.sem_inc(x_ready, 1)
            projected(H)
            do(dve.tensor_tensor(yq3[:, :, 0:H], yq3[:, :, 0:H], wide(vec["b1"][:, :]), ALU.add))
            do(dve.tensor_scalar(z3[:, :, 0:H], yq3[:, :, 0:H], 0.0, None, ALU.max))
            conv_table()
            summed(1)
            do(dve.tensor_copy(z3[:, :, H:W96], acc3[:, :, 0:H]))
            dve.sem_inc(x_ready, 1)
            projected(H)
            do(dve.tensor_tensor(yq3[:, :, 0:H], yq3[:, :, 0:H], wide(vec["b2"][:, :]), ALU.add))
            do(dve.tensor_tensor(xs3, xs3, yq3[:, :, 0:H], ALU.add))
            dve.wait_ge(emb_gathered, 32 * NB)
            At.turn = (L + 2) * NB7
            gated_table()
            gated(1, L + 3)
            gated_end(vec["gamma"][:, :], vec["beta"][:, :])
            do(dve.tensor_tensor(xs3, xs3, z3[:, :, 0:H], ALU.add))
            norm(xs3, z3[:, :, 0:H], relu=True)
            dve.sem_inc(degree_ready, 1)
            dve.wait_ge(degree_root, 1)
            do(dve.reciprocal(ln_d[:, 0:NB], deg[:, :]))
            do(dve.tensor_tensor(z3[:, :, 0:H], z3[:, :, 0:H], bc(ln_d[:, 0:NB]), ALU.mult))
            conv_table()
            summed(2)
            do(dve.tensor_tensor(z3[:, :, 0:H], z3[:, :, 0:H], acc3[:, :, 0:H], ALU.add))
            do(dve.tensor_tensor(z3[:, :, 0:H], z3[:, :, 0:H], bc(ln_d[:, 0:NB]), ALU.mult))
            dve.sem_inc(x_ready, 1)
            projected(H)
            do(dve.tensor_tensor(yq3[:, :, 0:H], yq3[:, :, 0:H], wide(vec["b3"][:, :]), ALU.add))
            do(dve.tensor_tensor(xs3, xs3, yq3[:, :, 0:H], ALU.add))
            dve.sem_inc(x_ready, 1)


_INS = ["x", "src", "dst", "edge_attr_40", "edge_weight", "node_type_119", "node_vec",
        "L0_gnn_Wq", "L0_gnn_gq", "L0_gnn_bq", "L0_gnn_Wk", "L0_gnn_gk", "L0_gnn_bk", "L0_gnn_Wu", "L0_gnn_go",
        "L0_gnn_bo", "L0_gnn_F1W", "L0_gnn_F1b", "L0_gnn_F2W", "L0_gnn_F2b", "L0_gnn_gn", "L0_gnn_bn", "L0_gnn_emb",
        "L1_gnn_w_rel1", "L1_gnn_w_root1", "L1_gnn_b1", "L1_gnn_w_rel2", "L1_gnn_w_root2", "L1_gnn_b2",
        "L2_gnn_b1", "L2_gnn_b2", "L2_gnn_emb", "L2_gnn_adaptW", "L2_gnn_gamma", "L2_gnn_beta", "L3_gnn_W", "L3_gnn_b"]
_TURNED = {"Wm_t": ("L0_gnn_Wm", (0, 2, 1)), "adapt_t": ("L0_gnn_adapt", (1, 0)),
           "W1_t": ("L2_gnn_W1", (1, 0)), "W2_t": ("L2_gnn_W2", (1, 0))}


def kernel(**inputs):
    import numpy as np
    import concourse.bacc as bacc
    from concourse.bass_utils import run_bass_kernel_spmd

    nc = bacc.Bacc("TRN2", target_bir_lowering=False, num_devices=1)
    laid = {n: np.ascontiguousarray(inputs[n]) for n in _INS}
    for n, (source, order) in _TURNED.items():
        laid[n] = np.ascontiguousarray(np.transpose(np.asarray(inputs[source]), order))
    aps = {n: nc.dram_tensor("in_" + n, v.shape, mybir.dt.from_np(v.dtype), kind="ExternalInput").ap()
           for n, v in laid.items()}
    out = nc.dram_tensor("out_0", (N, H), F32, kind="ExternalOutput").ap()
    build(nc, aps, out)
    r = run_bass_kernel_spmd(nc, [{"in_" + n: v for n, v in laid.items()}], core_ids=[0])
    return r.results[0]["out_0"]
```
